# Optimizing a Trainium2 kernel written in Bass

```python
import numpy as np
import jax
import jax.numpy as jnp

def _softmax(x, axis=-1):
    return jax.nn.softmax(x, axis=axis)

def _gelu(x):
    return jax.nn.gelu(x, approximate=True)

def _silu(x):
    return jax.nn.silu(x)

def _sigmoid(x):
    return jax.nn.sigmoid(x)

def _layernorm(x, axis=-1, eps=1e-05):
    m = jnp.mean(x, axis=axis, keepdims=True)
    v = jnp.var(x, axis=axis, keepdims=True)
    return (x - m) / jnp.sqrt(v + eps)

def _scatter_add(tgt, idx, src, axis=0):
    return tgt.at[idx].add(src)

def _segment_sum(src, seg, n):
    return jax.ops.segment_sum(src, seg, n)
kernel_name = 'mk_rec_standalone_d1_rec_r8_9eeb9f'

def setup_inputs(seed: int=0):
    np.random.seed(seed)
    _w = jnp.asarray

    def _rec_inputs():
        import jax
        import jax.numpy as jnp
        _rk = jax.random.key(seed)
        r_dx = -0.000171701 + 0.999137 * jax.random.normal(jax.random.fold_in(_rk, 1), (512, 13), jnp.float32)
        r_sx = jnp.stack([jax.random.randint(jax.random.fold_in(jax.random.fold_in(_rk, 2), 0), (512,), 86, 99990, jnp.int32), jax.random.randint(jax.random.fold_in(jax.random.fold_in(_rk, 2), 1), (512,), 10, 99946, jnp.int32), jax.random.randint(jax.random.fold_in(jax.random.fold_in(_rk, 2), 2), (512,), 78, 99986, jnp.int32), jax.random.randint(jax.random.fold_in(jax.random.fold_in(_rk, 2), 3), (512,), 62, 99977, jnp.int32), jax.random.randint(jax.random.fold_in(jax.random.fold_in(_rk, 2), 4), (512,), 1, 99988, jnp.int32), jax.random.randint(jax.random.fold_in(jax.random.fold_in(_rk, 2), 5), (512,), 1, 99988, jnp.int32), jax.random.randint(jax.random.fold_in(jax.random.fold_in(_rk, 2), 6), (512,), 18, 99973, jnp.int32), jax.random.randint(jax.random.fold_in(jax.random.fold_in(_rk, 2), 7), (512,), 17, 99988, jnp.int32), jax.random.randint(jax.random.fold_in(jax.random.fold_in(_rk, 2), 8), (512,), 44, 99975, jnp.int32), jax.random.randint(jax.random.fold_in(jax.random.fold_in(_rk, 2), 9), (512,), 28, 99998, jnp.int32), jax.random.randint(jax.random.fold_in(jax.random.fold_in(_rk, 2), 10), (512,), 5, 99993, jnp.int32), jax.random.randint(jax.random.fold_in(jax.random.fold_in(_rk, 2), 11), (512,), 32, 99985, jnp.int32), jax.random.randint(jax.random.fold_in(jax.random.fold_in(_rk, 2), 12), (512,), 51, 99951, jnp.int32), jax.random.randint(jax.random.fold_in(jax.random.fold_in(_rk, 2), 13), (512,), 129, 99982, jnp.int32), jax.random.randint(jax.random.fold_in(jax.random.fold_in(_rk, 2), 14), (512,), 3, 99966, jnp.int32), jax.random.randint(jax.random.fold_in(jax.random.fold_in(_rk, 2), 15), (512,), 15, 99987, jnp.int32), jax.random.randint(jax.random.fold_in(jax.random.fold_in(_rk, 2), 16), (512,), 22, 99998, jnp.int32), jax.random.randint(jax.random.fold_in(jax.random.fold_in(_rk, 2), 17), (512,), 31, 99949, jnp.int32), jax.random.randint(jax.random.fold_in(jax.random.fold_in(_rk, 2), 18), (512,), 15, 99996, jnp.int32), jax.random.randint(jax.random.fold_in(jax.random.fold_in(_rk, 2), 19), (512,), 6, 99942, jnp.int32), jax.random.randint(jax.random.fold_in(jax.random.fold_in(_rk, 2), 20), (512,), 28, 99986, jnp.int32), jax.random.randint(jax.random.fold_in(jax.random.fold_in(_rk, 2), 21), (512,), 10, 99991, jnp.int32), jax.random.randint(jax.random.fold_in(jax.random.fold_in(_rk, 2), 22), (512,), 7, 99965, jnp.int32), jax.random.randint(jax.random.fold_in(jax.random.fold_in(_rk, 2), 23), (512,), 15, 99963, jnp.int32), jax.random.randint(jax.random.fold_in(jax.random.fold_in(_rk, 2), 24), (512,), 29, 99990, jnp.int32), jax.random.randint(jax.random.fold_in(jax.random.fold_in(_rk, 2), 25), (512,), 42, 99986, jnp.int32)], axis=1)
        return (r_dx, r_sx)
    r_dx, r_sx = _rec_inputs()

    def _L0_rec_setup():
        import jax, jax.numpy as jnp
        import numpy as np
        B = 512
        F = 26
        V = 12500
        D = 64
        A = 64
        ND = 13
        FEA = ND + D
        HID = [FEA, 256, 128, 64]
        EPS = 1e-05

        def _afm_forward(sx, dx, emb_table, att_w_W, att_w_b, att_d_W, att_d_b, bn_gamma, bn_beta, w1, b1, w2, b2, w3, b3, wf, bf):
            embeds = emb_table[jnp.arange(F)[None, :], sx]
            i1, i2 = np.triu_indices(F, k=1)
            bi = embeds[:, i1, :] * embeds[:, i2, :]
            a = jax.nn.relu(jnp.einsum('bpd,da->bpa', bi, att_w_W) + att_w_b)
            scores = jnp.einsum('bpa,ao->bpo', a, att_d_W) + att_d_b
            w = jax.nn.softmax(scores, axis=1)
            att_out = jnp.sum(w * bi, axis=1)
            x = jnp.concatenate([att_out, dx], axis=-1)
            mu = jnp.mean(x, axis=0)
            var = jnp.mean((x - mu) ** 2, axis=0)
            x = (x - mu) * jax.lax.rsqrt(var + EPS) * bn_gamma + bn_beta
            x = jax.nn.relu(x @ w1 + b1)
            x = jax.nn.relu(x @ w2 + b2)
            x = jax.nn.relu(x @ w3 + b3)
            out = jax.nn.sigmoid(x @ wf + bf)
            return jnp.squeeze(out, axis=-1)
        key = jax.random.key(seed)
        ks = jax.random.split(key, 20)
        s = 0.05
        inp = {'sx': jax.random.randint(ks[0], (B, F), 0, V), 'dx': jax.random.normal(ks[1], (B, ND), dtype=jnp.float32), 'emb_table': jax.random.normal(ks[2], (F, V, D), dtype=jnp.float32) * s, 'att_w_W': jax.random.normal(ks[3], (D, A), dtype=jnp.float32) * s, 'att_w_b': jnp.zeros((A,), jnp.float32), 'att_d_W': jax.random.normal(ks[4], (A, 1), dtype=jnp.float32) * s, 'att_d_b': jnp.zeros((1,), jnp.float32), 'bn_gamma': jnp.ones((FEA,), jnp.float32), 'bn_beta': jnp.zeros((FEA,), jnp.float32), 'w1': jax.random.normal(ks[5], (HID[0], HID[1]), dtype=jnp.float32) * s, 'b1': jnp.zeros((HID[1],), jnp.float32), 'w2': jax.random.normal(ks[6], (HID[1], HID[2]), dtype=jnp.float32) * s, 'b2': jnp.zeros((HID[2],), jnp.float32), 'w3': jax.random.normal(ks[7], (HID[2], HID[3]), dtype=jnp.float32) * s, 'b3': jnp.zeros((HID[3],), jnp.float32), 'wf': jax.random.normal(ks[8], (HID[3], 1), dtype=jnp.float32) * s, 'bf': jnp.zeros((1,), jnp.float32)}
        return inp
    _L0_rec_all = _L0_rec_setup()
    _L0_rec_in = {k: v for k, v in _L0_rec_all.items() if k in ('emb_table', 'att_w_W', 'att_w_b', 'att_d_W', 'att_d_b', 'bn_gamma', 'bn_beta', 'w1', 'b1', 'w2', 'b2', 'w3', 'b3', 'wf', 'bf')}
    del _L0_rec_all
    return {'r_dx': r_dx, 'r_sx': r_sx, 'L0_rec_emb_table': _L0_rec_in['emb_table'], 'L0_rec_att_w_W': _L0_rec_in['att_w_W'], 'L0_rec_att_w_b': _L0_rec_in['att_w_b'], 'L0_rec_att_d_W': _L0_rec_in['att_d_W'], 'L0_rec_att_d_b': _L0_rec_in['att_d_b'], 'L0_rec_bn_gamma': _L0_rec_in['bn_gamma'], 'L0_rec_bn_beta': _L0_rec_in['bn_beta'], 'L0_rec_w1': _L0_rec_in['w1'], 'L0_rec_b1': _L0_rec_in['b1'], 'L0_rec_w2': _L0_rec_in['w2'], 'L0_rec_b2': _L0_rec_in['b2'], 'L0_rec_w3': _L0_rec_in['w3'], 'L0_rec_b3': _L0_rec_in['b3'], 'L0_rec_wf': _L0_rec_in['wf'], 'L0_rec_bf': _L0_rec_in['bf']}

def reference(r_dx, r_sx, L0_rec_emb_table, L0_rec_att_w_W, L0_rec_att_w_b, L0_rec_att_d_W, L0_rec_att_d_b, L0_rec_bn_gamma, L0_rec_bn_beta, L0_rec_w1, L0_rec_b1, L0_rec_w2, L0_rec_b2, L0_rec_w3, L0_rec_b3, L0_rec_wf, L0_rec_bf):
    import jax
    import jax.numpy as jnp

    def _L0_rec_ref(sx, dx, emb_table, att_w_W, att_w_b, att_d_W, att_d_b, bn_gamma, bn_beta, w1, b1, w2, b2, w3, b3, wf, bf):
        import jax, jax.numpy as jnp
        import numpy as np
        B = 512
        F = 26
        V = 12500
        D = 64
        A = 64
        ND = 13
        FEA = ND + D
        HID = [FEA, 256, 128, 64]
        EPS = 1e-05

        def _afm_forward(sx, dx, emb_table, att_w_W, att_w_b, att_d_W, att_d_b, bn_gamma, bn_beta, w1, b1, w2, b2, w3, b3, wf, bf):
            embeds = emb_table[jnp.arange(F)[None, :], sx]
            i1, i2 = np.triu_indices(F, k=1)
            bi = embeds[:, i1, :] * embeds[:, i2, :]
            a = jax.nn.relu(jnp.einsum('bpd,da->bpa', bi, att_w_W) + att_w_b)
            scores = jnp.einsum('bpa,ao->bpo', a, att_d_W) + att_d_b
            w = jax.nn.softmax(scores, axis=1)
            att_out = jnp.sum(w * bi, axis=1)
            x = jnp.concatenate([att_out, dx], axis=-1)
            mu = jnp.mean(x, axis=0)
            var = jnp.mean((x - mu) ** 2, axis=0)
            x = (x - mu) * jax.lax.rsqrt(var + EPS) * bn_gamma + bn_beta
            x = jax.nn.relu(x @ w1 + b1)
            x = jax.nn.relu(x @ w2 + b2)
            x = jax.nn.relu(x @ w3 + b3)
            out = jax.nn.sigmoid(x @ wf + bf)
            return jnp.squeeze(out, axis=-1)
        return _afm_forward(sx, dx, emb_table, att_w_W, att_w_b, att_d_W, att_d_b, bn_gamma, bn_beta, w1, b1, w2, b2, w3, b3, wf, bf)
    y = _L0_rec_ref(r_sx, r_dx, L0_rec_emb_table, L0_rec_att_w_W, L0_rec_att_w_b, L0_rec_att_d_W, L0_rec_att_d_b, L0_rec_bn_gamma, L0_rec_bn_beta, L0_rec_w1, L0_rec_b1, L0_rec_w2, L0_rec_b2, L0_rec_w3, L0_rec_b3, L0_rec_wf, L0_rec_bf)
    return y

_drawn_inputs = setup_inputs


def setup_inputs(seed=0):
    import zlib

    import numpy as np

    out = dict(_drawn_inputs(seed))
    spreads = {'L0_rec_att_w_b': (0.0, 0.8),
     'L0_rec_bn_gamma': (1.0, 0.6),
     'L0_rec_bn_beta': (0.0, 0.8),
     'L0_rec_b1': (0.0, 0.8),
     'L0_rec_b2': (0.0, 0.8),
     'L0_rec_b3': (0.0, 0.667)}
    factors = {'r_dx': 8.0,
     'L0_rec_emb_table': 8.0,
     'L0_rec_att_w_W': 8.0,
     'L0_rec_att_d_W': 8.0,
     'L0_rec_w1': 8.0,
     'L0_rec_w2': 8.0,
     'L0_rec_w3': 8.0,
     'L0_rec_wf': 6.318}
    for name, (base, spread) in spreads.items():
        noise = np.random.default_rng([zlib.crc32(name.encode()), seed]).standard_normal(out[name].shape)
        drawn = base * np.exp(spread * noise) if base else spread * noise
        out[name] = jnp.asarray(drawn.astype(out[name].dtype))
    for name, factor in factors.items():
        out[name] = (out[name] * factor).astype(out[name].dtype)
    return out
```

```python
import concourse.bass as bass
from concourse import mybir
from contextlib import ExitStack

F32 = mybir.dt.float32
I32 = mybir.dt.int32
ALU = mybir.AluOpType
ACT = mybir.ActivationFunctionType
AX = mybir.AxisListType

B, F, V, D, A, ND = 512, 26, 12500, 64, 64, 13
H1, H2, H3 = 256, 128, 64
FEA = D + ND
EPS = 1e-5
H, C, K, T = 2, 4, 16, 4
Q = 32
NDELTA = F // 2 - 1
NFULL = NDELTA * F
NPAIR = F * (F - 1) // 2
FW = F + NDELTA
U = K // 2
RING = 4
NB = 4
KB = K // NB
assert T * K * H * C == B and C * Q == 128 and H * D == 128 and NFULL + F // 2 == NPAIR


def afm_kernel(nc, dx, sx, table, att_w, att_wb, att_d, att_db, gamma, beta,
               w1, b1, w2, b2, w3, b3, wf, bf, out):
    with ExitStack() as ctx:
        def sb(name, shape, dt=F32):
            return ctx.enter_context(nc.sbuf_tensor(name, shape, dt))

        def ps(name, shape):
            return ctx.enter_context(nc.psum_tensor(name, shape, F32))

        def sem(name):
            return ctx.enter_context(nc.semaphore(name))

        ident = sb("ident", [128, 128])
        att_w_diag = sb("att_w_diag", [128, 128])
        att_bias = sb("att_bias", [128, 1])
        att_d_slide = sb("att_d_slide", [128, 2 * (K - 1) + Q])
        score_bias = sb("score_bias", [128, 1])
        w1_sb = sb("w1_sb", [FEA, H1])
        w2_sb = sb("w2_sb", [128, H1 // 128, H2])
        w3_sb = sb("w3_sb", [H2, H3])
        wf_sb = sb("wf_sb", [H3, 1])
        b1_sb = sb("b1_sb", [128, H1 // 128])
        b2_sb = sb("b2_sb", [H2, 1])
        b3_sb = sb("b3_sb", [H3, 1])
        bf_sb = sb("bf_sb", [1, 1])
        gamma_sb = sb("gamma_sb", [FEA, 1])
        beta_sb = sb("beta_sb", [FEA, 1])
        dx_rows = sb("dx_rows", [128, T, FEA])

        sx_raw = sb("sx_raw", [128, C, F], I32)
        field_base = sb("field_base", [128, F], I32)
        sx_f = sb("sx_f", [128, C, F])
        sx_wrap = sb("sx_wrap", [128, C, F])
        sx_pos = sb("sx_pos", [128, C, F])
        sx_clip = sb("sx_clip", [128, C, F])
        rows_f = sb("rows_f", [128, C, Q])
        rows_all = sb("rows_all", [128, 128], I32)
        rows_now = sb("rows_now", [128, K * H], I32)

        emb = sb("emb", [128, K, H, D])
        emb_keep = sb("emb_keep", [128, K, H, D])
        emb_t = sb("emb_t", [128, T * K, C, FW])
        prod = sb("prod", [128, RING, C, NPAIR])
        hid = sb("hid", [128, RING, C, NPAIR])
        neg_max = sb("neg_max", [128, 3])
        expd = sb("expd", [128, NPAIR])
        denom = sb("denom", [128, 2])
        att_skew = sb("att_skew", [128, F, FW])
        att_diag = sb("att_diag", [128, Q, C, F])
        pooled_i = sb("pooled_i", [128, 2, KB * C, F])
        pooled = sb("pooled", [128, T * K * C])

        feat = sb("feat", [FEA, B])
        bn_raw = sb("bn_raw", [FEA, 6])
        bn_mv = sb("bn_mv", [FEA, 2])
        bn_tmp = sb("bn_tmp", [FEA, 5])
        feat_n = sb("feat_n", [FEA, B])
        h1 = sb("h1", [128, H1 // 128, B])
        h2 = sb("h2", [H2, B])
        h3 = sb("h3", [H3, B])
        prob = sb("prob", [1, B])

        credit = sb("credit", [1, 3])
        z_ps = ps("z_ps", [128, C, 512])
        s_ps = ps("s_ps", [128, 512])
        tr_ps = ps("tr_ps", [128, 512])
        g_ps = ps("g_ps", [128, 512])
        x_ps = ps("x_ps", [128, 512])

        sx_loaded = sem("sx_loaded")
        consts_made = sem("consts_made")
        zeros_made = sem("zeros_made")
        att_loaded = sem("att_loaded")
        dense_loaded = sem("dense_loaded")
        rows_step = sem("rows_step")
        rows_turned = sem("rows_turned")
        rows_ready = sem("rows_ready")
        first_rows_here = sem("first_rows_here")
        rows_here = sem("rows_here")
        gathered = [sem(f"gathered{u}") for u in range(U)]
        kept = [sem(f"kept{u}") for u in range(U)]
        turned = sem("turned")
        emb_t_ready = sem("emb_t_ready")
        prod_ready = sem("prod_ready")
        z_ready = sem("z_ready")
        hid_ready = sem("hid_ready")
        scored = sem("scored")
        max_step = sem("max_step")
        exp_done = sem("exp_done")
        inv_done = sem("inv_done")
        skew_done = sem("skew_done")
        fold_done = sem("fold_done")
        diag_ready = sem("diag_ready")
        g_ready = sem("g_ready")
        g_used = sem("g_used")
        pooled_done = sem("pooled_done")
        dx_turned = sem("dx_turned")
        feat_ready = sem("feat_ready")
        bn_step = sem("bn_step")
        std_done = sem("std_done")
        feat_n_ready = sem("feat_n_ready")
        l1_done = sem("l1_done")
        h1_ready = sem("h1_ready")
        l2_done = sem("l2_done")
        h2_ready = sem("h2_ready")
        l3_done = sem("l3_done")
        h3_ready = sem("h3_ready")
        logit_done = sem("logit_done")
        prob_ready = sem("prob_ready")
        stored = sem("stored")
        N_ATT, N_DENSE = 16 * 7, 16 * 13

        def blocks(engine, body):
            body(0, True, False)
            with engine.Fori(1, T - 1) as t:
                body(t, False, False)
            body(T - 1, False, True)

        block = ctx.enter_context(nc.Block())

        @block.sync
        def _(sp):
            sp.dma_start(sx_raw[:, :, :], sx.rearrange("(g c) f -> g c f", c=C)).then_inc(sx_loaded, 16)
            sp.wait_ge(zeros_made, 2)
            for h in range(H):
                p = h * D
                sp.dma_start(att_w_diag[p:p + D, h * A:(h + 1) * A], att_w).then_inc(att_loaded, 16)
                sp.dma_start(att_d_slide[p:p + D, 2 * (K - 1) + h:2 * (K - 1) + h + 1],
                             att_d).then_inc(att_loaded, 16)
                sp.dma_start(att_bias[p:p + D, :], att_wb.rearrange("(a n) -> a n", n=1)).then_inc(att_loaded, 16)
            sp.dma_start(score_bias[:, :], att_db.partition_broadcast(128)).then_inc(att_loaded, 16)
            sp.dma_start(w1_sb[:, :], w1).then_inc(dense_loaded, 16)
            sp.dma_start(w2_sb[:, :, :], w2.rearrange("(m p) n -> p m n", p=128)).then_inc(dense_loaded, 16)
            sp.dma_start(w3_sb[:, :], w3).then_inc(dense_loaded, 16)
            sp.dma_start(wf_sb[:, :], wf).then_inc(dense_loaded, 16)
            for m in range(H1 // 128):
                sp.dma_start(b1_sb[:, m:m + 1],
                             b1[m * 128:(m + 1) * 128].rearrange("(p n) -> p n", n=1)).then_inc(dense_loaded, 16)
            sp.dma_start(b2_sb[:, :], b2.rearrange("(p n) -> p n", n=1)).then_inc(dense_loaded, 16)
            sp.dma_start(b3_sb[:, :], b3.rearrange("(p n) -> p n", n=1)).then_inc(dense_loaded, 16)
            sp.dma_start(bf_sb[:, :], bf.rearrange("(p n) -> p n", n=1)).then_inc(dense_loaded, 16)
            sp.dma_start(gamma_sb[:, :], gamma.rearrange("(p n) -> p n", n=1)).then_inc(dense_loaded, 16)
            sp.dma_start(beta_sb[:, :], beta.rearrange("(p n) -> p n", n=1)).then_inc(dense_loaded, 16)
            sp.wait_ge(zeros_made, 5)
            for hh in range(2):
                sp.dma_start(dx_rows[:, 2 * hh:2 * hh + 2, D:FEA],
                             dx.rearrange("(t p) n -> p t n", p=128)[:, 2 * hh:2 * hh + 2, :]).then_inc(dense_loaded, 16)

            def body(t, first, last):
                for u in range(U):
                    if first:
                        sp.wait_ge(turned, u + 1)
                    else:
                        sp.wait_ge(g_ready, (t - 1) * NB + (u // (U // NB) + 1))
                    sp.dma_start(emb_keep[:, 2 * u:2 * u + 2, :, :],
                                 emb[:, 2 * u:2 * u + 2, :, :]).then_inc(kept[u], 16)

            blocks(sp, body)
            sp.wait_ge(prob_ready, 1)
            sp.dma_start(out.rearrange("(a n) -> a n", a=1), prob[:, :]).then_inc(stored, 16)
            sp.wait_ge(stored, 16)

        @block.gpsimd
        def _(pool):
            nc.gpsimd.iota(field_base[:, :], pattern=[[V, F]], base=0, channel_multiplier=0).then_inc(consts_made, 1)
            nc.gpsimd.memset(ident[:, :], 0.0).then_inc(consts_made, 1)
            pool.wait_ge(consts_made, 2)
            nc.gpsimd.affine_select(out=ident[:, :], in_=ident[:, :], compare_op=ALU.not_equal, fill=1.0,
                                    base=0, pattern=[[-1, 128]], channel_multiplier=1).then_inc(consts_made, 1)

            def body(t, first, last):
                if first:
                    pool.wait_ge(rows_ready, 1)
                else:
                    for u in range(U):
                        pool.wait_ge(gathered[u], t * 64)
                    pool.wait_ge(kept[0], t * 16)
                nc.gpsimd.tensor_copy(rows_now[:, :], rows_all[:, bass.ds(t * (K * H), K * H)]).then_inc(
                    first_rows_here if first else rows_here, 16)
                pool.wait_ge(rows_ready, 1)
                if first:
                    pool.wait_ge(first_rows_here, 16)
                else:
                    pool.wait_ge(rows_here, t * 16)
                for k in range(K):
                    u = k // 2
                    if not first and k % 2 == 0 and k > 0:
                        pool.wait_ge(rows_ready, 1)
                        pool.wait_ge(kept[u], t * 16)
                    for h in range(H):
                        nc.gpsimd.indirect_dma_start(
                            emb[:, k, h, :], None, table.rearrange("f v d -> (f v) d"),
                            bass.IndirectOffsetOnAxis(ap=rows_now[:, k * H + h:k * H + h + 1], axis=0),
                        ).then_inc(gathered[u], 16)

            blocks(pool, body)

        @block.tensor
        def _(pe):
            def turn(t, u):
                pe.wait_ge(gathered[u], (t + 1) * 64)
                if not (isinstance(t, int) and t * U + u == 0):
                    pe.wait_ge(emb_t_ready, (t * U + u) * 2)
                for j in range(2):
                    last = nc.tensor.transpose(tr_ps[:, j * 128:(j + 1) * 128],
                                               emb[:, 2 * u + j, :, :].rearrange("p h d -> p (h d)"), ident[:, :])
                last.then_inc(turned, 1)

            def hidden(t, k):
                n = t * K + k
                pe.wait_ge(prod_ready, (n + 1) * 2)
                for c in range(C):
                    if c % 2 == 0 and not (isinstance(t, int) and t * K + k == 0):
                        pe.wait_ge(hid_ready, n * 2 + (c // 2 - 1))
                    mm = nc.tensor.matmul(z_ps[:, c, 0:NPAIR], att_w_diag[:, :], prod[:, k % RING, c, :],
                                          start=True, stop=True)
                    if c % 2 == 1:
                        mm.then_inc(z_ready, 1)

            def scores(t, k):
                n = t * K + k
                pe.wait_ge(hid_ready, (n + 1) * 2)
                if k == 0 and not (isinstance(t, int) and t == 0):
                    pe.wait_ge(exp_done, t)
                for c in range(C):
                    mm = nc.tensor.matmul(s_ps[Q * c:Q * (c + 1), 0:NPAIR],
                                          att_d_slide[:, 2 * (K - 1 - k):2 * (K - 1 - k) + Q],
                                          hid[:, k % RING, c, :], start=(k == 0), stop=(k == K - 1))
                mm.then_inc(scored, 1)

            def pool_batch(t, q, bank):
                if q == 0:
                    pe.wait_ge(diag_ready, (t + 1) * C)
                for u in range(q * (U // NB), (q + 1) * (U // NB)):
                    pe.wait_ge(kept[u], (t + 1) * 16)
                if not (isinstance(t, int) and bank is not g_ps):
                    pe.wait_ge(g_used, t * NB + (q + 2))
                for j in range(KB):
                    k = q * KB + j
                    for h in range(H):
                        mm = nc.tensor.matmul(bank[D * h:D * (h + 1), j * C * F:(j + 1) * C * F],
                                              emb_keep[:, k, h, :],
                                              att_diag[:, k * H + h, :, :].rearrange("p c i -> p (c i)"),
                                              start=True, stop=True)
                mm.then_inc(g_ready, 1)

            pe.wait_ge(consts_made, 3)
            pe.wait_ge(rows_step, 6)
            nc.tensor.transpose(x_ps[:, 0:128], rows_f[:, :, :].rearrange("p c j -> p (c j)"),
                                ident[:, :]).then_inc(rows_turned, 1)
            turn(0, 0)
            turn(0, 1)
            pe.wait_ge(att_loaded, N_ATT)

            def body(t, first, last):
                for k in range(K):
                    if k % 2 == 0:
                        u = k // 2 + 2
                        if u < U:
                            turn(t, u)
                        elif not last:
                            turn(t + 1, u - U)
                    hidden(t, k)
                    if k > 0:
                        scores(t, k - 1)
                    elif not first:
                        scores(t - 1, K - 1)
                    if not first and k >= 6 and (k - 6) % 2 == 0 and (k - 6) // 2 < NB:
                        pool_batch(t - 1, (k - 6) // 2, g_ps)

            blocks(pe, body)
            scores(T - 1, K - 1)
            pe.wait_ge(dense_loaded, N_DENSE)
            for t in range(T):
                mm = nc.tensor.transpose(x_ps[0:FEA, t * 128:(t + 1) * 128], dx_rows[:, t, :], ident[:, :])
            mm.then_inc(dx_turned, 1)
            for q in range(NB):
                pool_batch(T - 1, q, g_ps if q == 0 else z_ps[:, q, :])
            pe.wait_ge(feat_n_ready, 1)
            for m in range(H1 // 128):
                nc.tensor.matmul(z_ps[:, m, :], w1_sb[:, m * 128:(m + 1) * 128], feat_n[:, :],
                                 start=True, stop=True).then_inc(l1_done, 1)
            for m in range(H1 // 128):
                pe.wait_ge(h1_ready, m + 1)
                mm = nc.tensor.matmul(z_ps[:, 2, :], w2_sb[:, m, :], h1[:, m, :],
                                      start=(m == 0), stop=(m == H1 // 128 - 1))
            mm.then_inc(l2_done, 1)
            pe.wait_ge(h2_ready, 1)
            nc.tensor.matmul(z_ps[0:H3, 3, :], w3_sb[:, :], h2[:, :], start=True, stop=True).then_inc(l3_done, 1)
            pe.wait_ge(h3_ready, 1)
            nc.tensor.matmul(g_ps[0:1, :], wf_sb[:, :], h3[:, :], start=True, stop=True).then_inc(logit_done, 1)

        @block.scalar
        def _(act):
            def exponentials(t):
                act.wait_ge(max_step, (t + 1) * 3)
                act.wait_ge(skew_done, t * 2 + 2)
                nc.scalar.activation(expd[:, :], s_ps[:, 0:NPAIR], ACT.Exp, bias=neg_max[:, 2:3], scale=1.0,
                                     accum_out=denom[:, 0:1]).then_inc(exp_done, 1)

            def body(t, first, last):
                if first:
                    act.wait_ge(att_loaded, N_ATT)
                for k in range(K):
                    n = t * K + k
                    if not (first and k < RING):
                        act.wait_ge(scored, n - (RING - 1))
                    for half in range(2):
                        act.wait_ge(z_ready, n * 2 + (half + 1))
                        nc.scalar.activation(hid[:, k % RING, 2 * half:2 * half + 2, :],
                                             z_ps[:, 2 * half:2 * half + 2, 0:NPAIR], ACT.Relu,
                                             bias=att_bias[:, :], scale=1.0).then_inc(hid_ready, 1)
                        if not first and k == 1 and half == 0:
                            exponentials(t - 1)

            blocks(act, body)
            exponentials(T - 1)
            act.wait_ge(bn_step, 3)
            nc.scalar.activation(bn_tmp[:, 1:2], bn_tmp[:, 0:1], ACT.Sqrt).then_inc(std_done, 1)
            act.wait_ge(l1_done, 1)
            nc.scalar.activation(h1[:, 0, :], z_ps[:, 0, :], ACT.Relu, bias=b1_sb[:, 0:1], scale=1.0).then_inc(h1_ready, 1)
            act.wait_ge(logit_done, 1)
            nc.scalar.activation(prob[:, :].rearrange("a (n h c) -> a h n c", h=H, c=C),
                                 g_ps[0:1, :].rearrange("a (h n c) -> a h n c", h=H, c=C), ACT.Sigmoid,
                                 bias=bf_sb[:, :], scale=1.0).then_inc(prob_ready, 1)

        @block.vector
        def _(dve):
            dve_zero = [(att_w_diag[:, :], 1), (att_d_slide[:, :], 1), (att_skew[:, :, :], 1),
                        (att_diag[:, :, :, :], 1), (dx_rows[:, :, 0:D], 1)]
            for i, credited in enumerate((g_used, skew_done, pooled_done)):
                nc.vector.memset(credit[:, i:i + 1], 0.0).then_inc(credited, 2)
            for tile, n in dve_zero[:2]:
                nc.vector.memset(tile, 0.0).then_inc(zeros_made, n)
            dve.wait_ge(sx_loaded, 16)
            dve.wait_ge(consts_made, 1)
            nc.vector.tensor_copy(sx_f[:, :, :], sx_raw[:, :, :]).then_inc(rows_step, 1)
            dve.wait_ge(rows_step, 1)
            nc.vector.tensor_scalar(sx_wrap[:, :, :], sx_f[:, :, :], 0.0, float(V), ALU.is_lt, ALU.mult).then_inc(rows_step, 1)
            dve.wait_ge(rows_step, 2)
            nc.vector.tensor_tensor(sx_pos[:, :, :], sx_f[:, :, :], sx_wrap[:, :, :], ALU.add).then_inc(rows_step, 1)
            dve.wait_ge(rows_step, 3)
            nc.vector.tensor_scalar(sx_clip[:, :, :], sx_pos[:, :, :], 0.0, float(V - 1), ALU.max, ALU.min).then_inc(rows_step, 1)
            dve.wait_ge(rows_step, 4)
            base = field_base[:, :].rearrange("p (a f) -> p a f", a=1).broadcast_to([128, C, F])
            nc.vector.tensor_tensor(rows_f[:, :, 0:F], sx_clip[:, :, :], base, ALU.add).then_inc(rows_step, 1)
            dve.wait_ge(rows_step, 5)
            nc.vector.tensor_copy(rows_f[:, :, F:Q], rows_f[:, :, 0:Q - F]).then_inc(rows_step, 1)
            dve.wait_ge(rows_turned, 1)
            nc.vector.tensor_copy(rows_all[:, :], x_ps[:, 0:128]).then_inc(rows_ready, 1)
            for tile, n in dve_zero[2:]:
                nc.vector.memset(tile, 0.0).then_inc(zeros_made, n)

            def spread(t, u):
                dve.wait_ge(turned, t * U + (u + 1))
                src = tr_ps[:, 0:2 * 128].rearrange("p (x j) -> p x j", j=Q)
                dst = emb_t[:, bass.ds(t * K + 2 * u, 2), :, :].rearrange("p n c j -> p (n c) j")
                nc.vector.tensor_copy(dst[:, :, 0:Q], src).then_inc(emb_t_ready, 1)
                nc.vector.tensor_copy(dst[:, :, Q:FW], src[:, :, Q - F:FW - F]).then_inc(emb_t_ready, 1)

            def products(t, k):
                n = t * K + k
                if k % 2 == 0:
                    dve.wait_ge(emb_t_ready, (t * U + (k // 2 + 1)) * 2)
                if not (isinstance(t, int) and t * K + k < RING):
                    dve.wait_ge(z_ready, (n - (RING - 1)) * 2)
                e = emb_t[:, bass.ds(n, 1), :, :].rearrange("p n c j -> p (n c) j")
                row = list(e.ap)
                part, step_c = row[0], row[1]
                left = bass.AP(e.tensor, e.offset, [part, step_c, [0, NDELTA], [1, F]])
                right = bass.AP(e.tensor, e.offset + 1, [part, step_c, [1, NDELTA], [1, F]])
                slot = prod[:, k % RING, :, :]
                nc.vector.tensor_tensor(slot[:, :, 0:NFULL].rearrange("p c (s i) -> p c s i", i=F), left, right,
                                        ALU.mult).then_inc(prod_ready, 1)
                nc.vector.tensor_tensor(slot[:, :, NFULL:NPAIR], e[:, :, 0:F // 2], e[:, :, F // 2:F],
                                        ALU.mult).then_inc(prod_ready, 1)

            def maxima(t):
                dve.wait_ge(scored, (t + 1) * K)
                nc.vector.reduce_max(neg_max[:, 0:1], s_ps[:, 0:NPAIR], AX.X).then_inc(max_step, 1)
                dve.wait_ge(max_step, t * 3 + 1)
                nc.vector.tensor_tensor(neg_max[:, 1:2], neg_max[:, 0:1], score_bias[:, :], ALU.add).then_inc(max_step, 1)
                dve.wait_ge(max_step, t * 3 + 2)
                nc.vector.tensor_tensor(neg_max[:, 2:3], score_bias[:, :], neg_max[:, 1:2], ALU.subtract).then_inc(max_step, 1)

            def weights(t):
                dve.wait_ge(exp_done, t + 1)
                nc.vector.reciprocal(denom[:, 1:2], denom[:, 0:1]).then_inc(inv_done, 1)
                dve.wait_ge(inv_done, t + 1)
                base = att_skew[:, :, :]
                part = list(base.ap)[0]
                full = bass.AP(base.tensor, base.offset + 1, [part, [1, NDELTA], [FW + 1, F]])
                half = bass.AP(base.tensor, base.offset + F // 2, [part, [FW + 1, F // 2]])
                nc.vector.tensor_scalar(full, expd[:, 0:NFULL].rearrange("p (s i) -> p s i", i=F),
                                        denom[:, 1:2], None, ALU.mult).then_inc(skew_done, 1)
                nc.vector.tensor_scalar(half, expd[:, NFULL:NPAIR], denom[:, 1:2], None, ALU.mult).then_inc(skew_done, 1)
                dve.wait_ge(skew_done, (t + 1) * 2 + 2)
                lo = Q - NDELTA
                nc.vector.tensor_copy(att_skew[:, lo:F, Q - F:FW - F], att_skew[:, lo:F, Q:FW]).then_inc(fold_done, 1)

            def diagonal(t, c):
                if c == 0:
                    dve.wait_ge(fold_done, t + 1)
                    dve.wait_ge(g_used, t * NB + 2)
                quad = slice(Q * c, Q * (c + 1))
                nc.vector.transpose(att_diag[quad, :, c, :].rearrange("p m i -> p i m"),
                                    att_skew[quad, :, 0:Q]).then_inc(diag_ready, 1)

            def pooling(t, q, bank):
                dve.wait_ge(g_ready, t * NB + (q + 1))
                dve.wait_ge(pooled_done, t * NB + (q + 1))
                e = emb_t[:, bass.ds(t * K + q * KB, KB), :, 0:F].rearrange("p n c j -> p (n c) j")
                nc.vector.tensor_tensor(pooled_i[:, q % 2, :, :], bank[:, 0:KB * C * F].rearrange("p (x i) -> p x i", i=F), e,
                                        ALU.mult).then_inc(g_used, 1)
                dve.wait_ge(g_used, t * NB + (q + 3))
                nc.vector.tensor_reduce(pooled[:, bass.ds(t * (K * C) + q * (KB * C), KB * C)], pooled_i[:, q % 2, :, :],
                                        AX.X, ALU.add).then_inc(pooled_done, 1)

            def body(t, first, last):
                for k in range(K):
                    if k % 2 == 0:
                        spread(t, k // 2)
                    products(t, k)
                    if first:
                        continue
                    if k == 2:
                        maxima(t - 1)
                    elif k == 3:
                        weights(t - 1)
                    elif k in (4, 5):
                        diagonal(t - 1, 2 * (k - 4))
                        diagonal(t - 1, 2 * (k - 4) + 1)
                    elif k >= 8 and k % 2 == 0:
                        pooling(t - 1, (k - 8) // 2, g_ps)

            blocks(dve, body)
            maxima(T - 1)
            dve.wait_ge(dx_turned, 1)
            nc.vector.tensor_copy(feat[D:FEA, :].rearrange("p (h n c) -> p h n c", h=H, c=C),
                                  x_ps[D:FEA, :].rearrange("p (n h c) -> p h n c", h=H, c=C)).then_inc(feat_ready, 1)
            weights(T - 1)
            for c in range(C):
                diagonal(T - 1, c)
            for q in range(NB):
                pooling(T - 1, q, g_ps if q == 0 else z_ps[:, q, :])
            dve.wait_ge(pooled_done, T * NB + 2)
            for h in range(H):
                nc.vector.tensor_copy(feat[0:D, h * (B // H):(h + 1) * (B // H)],
                                      pooled[h * D:(h + 1) * D, :]).then_inc(feat_ready, 1)
            dve.wait_ge(feat_ready, 3)
            nc.vector.bn_stats(bn_raw[:, :], feat[:, :]).then_inc(bn_step, 1)
            dve.wait_ge(bn_step, 1)
            nc.vector.bn_aggr(bn_mv[:, :], bn_raw[:, :]).then_inc(bn_step, 1)
            dve.wait_ge(bn_step, 2)
            nc.vector.tensor_scalar(bn_tmp[:, 0:1], bn_mv[:, 1:2], EPS, None, ALU.add).then_inc(bn_step, 1)
            dve.wait_ge(std_done, 1)
            dve.wait_ge(dense_loaded, N_DENSE)
            nc.vector.reciprocal(bn_tmp[:, 2:3], bn_tmp[:, 1:2]).then_inc(bn_step, 1)
            dve.wait_ge(bn_step, 4)
            nc.vector.tensor_tensor(bn_tmp[:, 3:4], bn_tmp[:, 2:3], gamma_sb[:, :], ALU.mult).then_inc(bn_step, 1)
            dve.wait_ge(bn_step, 5)
            nc.vector.tensor_tensor(bn_mv[:, 1:2], bn_mv[:, 0:1], bn_tmp[:, 3:4], ALU.mult).then_inc(bn_step, 1)
            dve.wait_ge(bn_step, 6)
            nc.vector.tensor_tensor(bn_tmp[:, 4:5], beta_sb[:, :], bn_mv[:, 1:2], ALU.subtract).then_inc(bn_step, 1)
            dve.wait_ge(bn_step, 7)
            nc.vector.tensor_scalar(feat_n[:, :], feat[:, :], bn_tmp[:, 3:4], bn_tmp[:, 4:5], ALU.mult,
                                    ALU.add).then_inc(feat_n_ready, 1)

            def relu_bias(dst, src, bias, ready):
                nc.vector.tensor_scalar(dst, src, bias, 0.0, ALU.add, ALU.max).then_inc(ready, 1)

            dve.wait_ge(l1_done, 2)
            dve.wait_ge(h1_ready, 1)
            relu_bias(h1[:, 1, :], z_ps[:, 1, :], b1_sb[:, 1:2], h1_ready)
            dve.wait_ge(l2_done, 1)
            relu_bias(h2[:, :], z_ps[:, 2, :], b2_sb[:, :], h2_ready)
            dve.wait_ge(l3_done, 1)
            relu_bias(h3[:, :], z_ps[0:H3, 3, :], b3_sb[:, :], h3_ready)


_INS = ['r_dx', 'r_sx', 'L0_rec_emb_table', 'L0_rec_att_w_W', 'L0_rec_att_w_b', 'L0_rec_att_d_W',
        'L0_rec_att_d_b', 'L0_rec_bn_gamma', 'L0_rec_bn_beta', 'L0_rec_w1', 'L0_rec_b1', 'L0_rec_w2',
        'L0_rec_b2', 'L0_rec_w3', 'L0_rec_b3', 'L0_rec_wf', 'L0_rec_bf']


def kernel(**inputs):
    import numpy as np
    import concourse.bacc as bacc
    from concourse.bass_utils import run_bass_kernel_spmd

    nc = bacc.Bacc("TRN2", target_bir_lowering=False, num_devices=1)
    arrays, args = {}, []
    for name in _INS:
        a = np.ascontiguousarray(inputs[name])
        arrays[f"in_{name}"] = a
        args.append(nc.dram_tensor(f"in_{name}", a.shape, mybir.dt.from_np(a.dtype), kind="ExternalInput").ap())
    args.append(nc.dram_tensor("out_prob", (B,), F32, kind="ExternalOutput").ap())
    afm_kernel(nc, *args)
    r = run_bass_kernel_spmd(nc, [arrays], core_ids=[0])
    return r.results[0]["out_prob"]
```

```python
import concourse.bass as bass
from concourse import mybir
from contextlib import ExitStack

F32 = mybir.dt.float32
I32 = mybir.dt.int32
ALU = mybir.AluOpType
ACT = mybir.ActivationFunctionType
AX = mybir.AxisListType

B, F, V, D, A, ND = 512, 26, 12500, 64, 64, 13
H1, H2, H3 = 256, 128, 64
FEA = D + ND
EPS = 1e-5
H, C, K, T = 2, 4, 16, 4
BH = B // H
Q = 32
NDELTA = F // 2 - 1
NFULL = NDELTA * F
NPAIR = F * (F - 1) // 2
FW = F + NDELTA
U = K // 2
RING = 4
NB = 4
KB = K // NB
assert T * K * H * C == B and C * Q == 128 and H * D == 128 and NFULL + F // 2 == NPAIR


def afm_kernel(nc, dx, sx, table, att_w, att_wb, att_d, att_db, gamma, beta,
               w1, b1, w2, b2, w3, b3, wf, bf, out):
    with ExitStack() as ctx:
        def sb(name, shape, dt=F32):
            return ctx.enter_context(nc.sbuf_tensor(name, shape, dt))

        def ps(name, shape):
            return ctx.enter_context(nc.psum_tensor(name, shape, F32))

        def sem(name):
            return ctx.enter_context(nc.semaphore(name))

        ident = sb("ident", [128, 128])
        att_w_diag = sb("att_w_diag", [128, 128])
        att_bias = sb("att_bias", [128, 1])
        att_d_slide = sb("att_d_slide", [128, 2 * (K - 1) + Q])
        score_bias = sb("score_bias", [128, 1])
        w1_sb = sb("w1_sb", [FEA, H1])
        w2_sb = sb("w2_sb", [128, H1 // 128, H2])
        w3_sb = sb("w3_sb", [H2, H3])
        wf_sb = sb("wf_sb", [H3, 1])
        b1_sb = sb("b1_sb", [128, H1 // 128])
        b2_sb = sb("b2_sb", [H2, 1])
        b3_sb = sb("b3_sb", [H3, 1])
        bf_sb = sb("bf_sb", [1, 1])
        gamma_sb = sb("gamma_sb", [FEA, 1])
        beta_sb = sb("beta_sb", [FEA, 1])
        eps_sb = sb("eps_sb", [FEA, 1])
        dx_rows = sb("dx_rows", [128, T, FEA])

        sx_raw = sb("sx_raw", [128, C, F], I32)
        field_base = sb("field_base", [128, F], I32)
        sx_wrap = sb("sx_wrap", [128, C, F])
        sx_pos = sb("sx_pos", [128, C, F])
        sx_clip = sb("sx_clip", [128, C, F])
        rows_f = sb("rows_f", [128, C, Q])
        rows_all = sb("rows_all", [128, 128], I32)
        rows_now = sb("rows_now", [128, K * H], I32)

        emb = sb("emb", [128, K, H, D])
        emb_keep = sb("emb_keep", [128, K, H, D])
        emb_t = sb("emb_t", [128, T * K, C, FW])
        prod = sb("prod", [128, RING, C, NPAIR])
        hid = sb("hid", [128, RING, C, NPAIR])
        neg_max = sb("neg_max", [128, 3])
        expd = sb("expd", [128, NPAIR])
        denom = sb("denom", [128, 2])
        att_skew = sb("att_skew", [128, F, FW])
        att_compact = sb("att_compact", [128, F, Q])
        att_diag = sb("att_diag", [128, Q, C, F])
        pooled_i = sb("pooled_i", [128, 2, KB * C, F])
        pooled = sb("pooled", [128, T * K * C])

        feat = sb("feat", [FEA, B])
        bn_raw = sb("bn_raw", [FEA, T * H, 6])
        bn_mv = sb("bn_mv", [FEA, 2])
        bn_tmp = sb("bn_tmp", [FEA, 5])
        feat_n = sb("feat_n", [FEA, B])
        h1 = sb("h1", [128, H1 // 128, B])
        h2 = sb("h2", [H2, B])
        h3 = sb("h3", [H3, B])
        prob = sb("prob", [1, B])

        credit = sb("credit", [1, 3])
        z_ps = ps("z_ps", [128, C, 512])
        s_ps = ps("s_ps", [128, 512])
        tr_ps = ps("tr_ps", [128, 512])
        g_ps = ps("g_ps", [128, 512])
        x_ps = ps("x_ps", [128, 512])
        l2_ps, l3_ps = (g_ps, tr_ps), (x_ps, s_ps)

        sx_loaded = sem("sx_loaded")
        consts_made = sem("consts_made")
        zeros_made = sem("zeros_made")
        att_loaded = sem("att_loaded")
        dense_loaded = sem("dense_loaded")
        rows_step = sem("rows_step")
        rows_turned = sem("rows_turned")
        rows_ready = sem("rows_ready")
        rows_here = sem("rows_here")
        gathered = [sem(f"gathered{u}") for u in range(U)]
        kept = [sem(f"kept{u}") for u in range(U)]
        first_gathered = sem("first_gathered")
        first_turned = sem("first_turned")
        first_emb_t_ready = sem("first_emb_t_ready")
        turned = sem("turned")
        emb_t_ready = sem("emb_t_ready")
        prod_ready = sem("prod_ready")
        z_ready = sem("z_ready")
        hid_ready = sem("hid_ready")
        scored = sem("scored")
        max_step = sem("max_step")
        exp_done = sem("exp_done")
        inv_done = sem("inv_done")
        skew_done = sem("skew_done")
        fold_done = sem("fold_done")
        diag_ready = sem("diag_ready")
        compact_ready = sem("compact_ready")
        spread_ready = [sem(f"spread_ready{half}") for half in range(2)]
        g_ready = sem("g_ready")
        g_used = sem("g_used")
        pooled_done = sem("pooled_done")
        dx_turned = sem("dx_turned")
        feat_ready = sem("feat_ready")
        stats_done = sem("stats_done")
        bn_step = sem("bn_step")
        neg_mean = sem("neg_mean")
        std_done = sem("std_done")
        feat_n_ready = [sem(f"feat_n_ready{h}") for h in range(H)]
        l1_done = [sem(f"l1_done{h}") for h in range(H)]
        h1_ready = [[sem(f"h1_ready{h}{m}") for m in range(H1 // 128)] for h in range(H)]
        l2_done = [sem(f"l2_done{h}") for h in range(H)]
        h2_ready = [sem(f"h2_ready{h}") for h in range(H)]
        l3_done = [sem(f"l3_done{h}") for h in range(H)]
        h3_ready = [sem(f"h3_ready{h}") for h in range(H)]
        logit_done = [sem(f"logit_done{h}") for h in range(H)]
        prob_ready = sem("prob_ready")
        stored = sem("stored")
        POOL_ROUNDS = [6, 8, 10, 12]
        WARM_SOFTMAX, WARM_NORM = 16, 10
        N_ATT, N_DENSE = 16 * 7, 16 * 13

        def landed(t, u):
            return (t + 1) * 64 - 32 if u == 0 else (t + 1) * 64

        def blocks(engine, body):
            body(0, True, False)
            with engine.Fori(1, T - 1) as t:
                body(t, False, False)
            body(T - 1, False, True)

        def spread_diagonal(engine, c, copy):
            engine.wait_ge(compact_ready, 1)
            quad = slice(Q * c, Q * (c + 1))
            for half in range(2):
                rows = slice(half * (Q // 2), (half + 1) * (Q // 2))
                copy(att_diag[quad, rows, c, :].rearrange("p m i -> p i m"),
                     att_compact[quad, :, rows]).then_inc(spread_ready[half], 1)

        block = ctx.enter_context(nc.Block())

        @block.sync
        def _(sp):
            sp.dma_start(sx_raw[:, :, :], sx.rearrange("(g c) f -> g c f", c=C)).then_inc(sx_loaded, 16)
            sp.wait_ge(zeros_made, 2)
            for h in range(H):
                p = h * D
                sp.dma_start(att_w_diag[p:p + D, h * A:(h + 1) * A], att_w).then_inc(att_loaded, 16)
                sp.dma_start(att_d_slide[p:p + D, 2 * (K - 1) + h:2 * (K - 1) + h + 1],
                             att_d).then_inc(att_loaded, 16)
                sp.dma_start(att_bias[p:p + D, :], att_wb.rearrange("(a n) -> a n", n=1)).then_inc(att_loaded, 16)
            sp.dma_start(score_bias[:, :], att_db.partition_broadcast(128)).then_inc(att_loaded, 16)
            sp.dma_start(w1_sb[:, :], w1).then_inc(dense_loaded, 16)
            sp.dma_start(w2_sb[:, :, :], w2.rearrange("(m p) n -> p m n", p=128)).then_inc(dense_loaded, 16)
            sp.dma_start(w3_sb[:, :], w3).then_inc(dense_loaded, 16)
            sp.dma_start(wf_sb[:, :], wf).then_inc(dense_loaded, 16)
            for m in range(H1 // 128):
                sp.dma_start(b1_sb[:, m:m + 1],
                             b1[m * 128:(m + 1) * 128].rearrange("(p n) -> p n", n=1)).then_inc(dense_loaded, 16)
            sp.dma_start(b2_sb[:, :], b2.rearrange("(p n) -> p n", n=1)).then_inc(dense_loaded, 16)
            sp.dma_start(b3_sb[:, :], b3.rearrange("(p n) -> p n", n=1)).then_inc(dense_loaded, 16)
            sp.dma_start(bf_sb[:, :], bf.rearrange("(p n) -> p n", n=1)).then_inc(dense_loaded, 16)
            sp.dma_start(gamma_sb[:, :], gamma.rearrange("(p n) -> p n", n=1)).then_inc(dense_loaded, 16)
            sp.dma_start(beta_sb[:, :], beta.rearrange("(p n) -> p n", n=1)).then_inc(dense_loaded, 16)
            sp.wait_ge(zeros_made, 3)
            for hh in range(2):
                sp.dma_start(dx_rows[:, 2 * hh:2 * hh + 2, D:FEA],
                             dx.rearrange("(t p) n -> p t n", p=128)[:, 2 * hh:2 * hh + 2, :]).then_inc(dense_loaded, 16)

            def body(t, first, last):
                for u in range(U):
                    if first:
                        sp.wait_ge(turned, u + 1)
                    else:
                        sp.wait_ge(g_ready, (t - 1) * NB + (u // (U // NB) + 1))
                    sp.dma_start(emb_keep[:, 2 * u:2 * u + 2, :, :],
                                 emb[:, 2 * u:2 * u + 2, :, :]).then_inc(kept[u], 16)

            blocks(sp, body)
            sp.wait_ge(prob_ready, H)
            sp.dma_start(out.rearrange("(a n) -> a n", a=1), prob[:, :]).then_inc(stored, 16)
            sp.wait_ge(stored, 16)

        @block.gpsimd
        def _(pool):
            nc.gpsimd.iota(field_base[:, :], pattern=[[V, F]], base=0, channel_multiplier=0).then_inc(consts_made, 1)
            nc.gpsimd.memset(ident[:, :], 0.0).then_inc(consts_made, 1)
            nc.gpsimd.memset(eps_sb[:, :], EPS).then_inc(consts_made, 1)
            pool.wait_ge(consts_made, 3)
            nc.gpsimd.affine_select(out=ident[:, :], in_=ident[:, :], compare_op=ALU.not_equal, fill=1.0,
                                    base=0, pattern=[[-1, 128]], channel_multiplier=1).then_inc(consts_made, 1)

            def body(t, first, last):
                if first:
                    pool.wait_ge(rows_ready, 1)
                else:
                    for u in range(U):
                        pool.wait_ge(gathered[u], landed(t - 1, u))
                    pool.wait_ge(rows_ready, 2)
                    pool.wait_ge(kept[0], t * 16)
                    nc.gpsimd.tensor_copy(rows_now[:, :], rows_all[:, bass.ds(t * (K * H), K * H)]).then_inc(rows_here, 16)
                    pool.wait_ge(rows_ready, 2)
                    pool.wait_ge(rows_here, t * 16)
                for k in range(K):
                    u = k // 2
                    if not first and k % 2 == 0 and k > 0:
                        pool.wait_ge(rows_ready, 2)
                        pool.wait_ge(kept[u], t * 16)
                    for h in range(H):
                        nc.gpsimd.indirect_dma_start(
                            emb[:, k, h, :], None, table.rearrange("f v d -> (f v) d"),
                            bass.IndirectOffsetOnAxis(ap=rows_now[:, k * H + h:k * H + h + 1], axis=0),
                        ).then_inc(first_gathered if first and k == 0 else gathered[u], 16)

            blocks(pool, body)
            spread_diagonal(pool, C - 2, nc.gpsimd.tensor_copy)

        @block.tensor
        def _(pe):
            def turn(t, u):
                pe.wait_ge(gathered[u], landed(t, u))
                if not (isinstance(t, int) and t * U + u == 0):
                    pe.wait_ge(emb_t_ready, (t * U + u) * 2)
                for j in range(2):
                    last = nc.tensor.transpose(tr_ps[:, j * 128:(j + 1) * 128],
                                               emb[:, 2 * u + j, :, :].rearrange("p h d -> p (h d)"), ident[:, :])
                last.then_inc(turned, 1)

            def hidden(t, k):
                n = t * K + k
                pe.wait_ge(prod_ready, (n + 1) * 2)
                for c in range(C):
                    if c % 2 == 0 and not (isinstance(t, int) and t * K + k == 0):
                        pe.wait_ge(hid_ready, n * 2 + (c // 2 - 1))
                    mm = nc.tensor.matmul(z_ps[:, c, 0:NPAIR], att_w_diag[:, :], prod[:, k % RING, c, :],
                                          start=True, stop=True)
                    if c % 2 == 1:
                        mm.then_inc(z_ready, 1)

            def scores(t, k):
                n = t * K + k
                pe.wait_ge(hid_ready, (n + 1) * 2)
                if k == 0 and not (isinstance(t, int) and t == 0):
                    pe.wait_ge(exp_done, t)
                for c in range(C):
                    mm = nc.tensor.matmul(s_ps[Q * c:Q * (c + 1), 0:NPAIR],
                                          att_d_slide[:, 2 * (K - 1 - k):2 * (K - 1 - k) + Q],
                                          hid[:, k % RING, c, :], start=(k == 0), stop=(k == K - 1))
                mm.then_inc(scored, 1)

            def pool_batch(t, q, bank, final=False):
                if final:
                    if q % 2 == 0:
                        pe.wait_ge(spread_ready[q // 2], C)
                elif q == 0:
                    pe.wait_ge(diag_ready, (t + 1) * C)
                for u in range(q * (U // NB), (q + 1) * (U // NB)):
                    pe.wait_ge(kept[u], (t + 1) * 16)
                if not (isinstance(t, int) and bank is not g_ps):
                    pe.wait_ge(g_used, t * NB + (q + 2))
                for j in range(KB):
                    k = q * KB + j
                    for h in range(H):
                        mm = nc.tensor.matmul(bank[D * h:D * (h + 1), j * C * F:(j + 1) * C * F],
                                              emb_keep[:, k, h, :],
                                              att_diag[:, k * H + h, :, :].rearrange("p c i -> p (c i)"),
                                              start=True, stop=True)
                mm.then_inc(g_ready, 1)

            def turn_dx():
                pe.wait_ge(dense_loaded, N_DENSE)
                pe.wait_ge(first_emb_t_ready, 2)
                for t in range(T):
                    mm = nc.tensor.transpose(x_ps[0:FEA, t * 128:(t + 1) * 128], dx_rows[:, t, :], ident[:, :])
                mm.then_inc(dx_turned, 1)

            def keep_warm(n):
                for _ in range(n):
                    nc.tensor.matmul(x_ps[:, 0:128], ident[:, :], ident[:, :], start=True, stop=True)

            pe.wait_ge(consts_made, 4)
            pe.wait_ge(rows_step, 5)
            nc.tensor.transpose(x_ps[:, 0:128], rows_f[:, :, :].rearrange("p c j -> p (c j)"),
                                ident[:, :]).then_inc(rows_turned, 1)
            pe.wait_ge(rows_ready, 2)
            pe.wait_ge(first_gathered, 32)
            nc.tensor.transpose(x_ps[:, 0:128], emb[:, 0, :, :].rearrange("p h d -> p (h d)"),
                                ident[:, :]).then_inc(first_turned, 1)
            pe.wait_ge(gathered[0], 32)
            nc.tensor.transpose(tr_ps[:, 128:256], emb[:, 1, :, :].rearrange("p h d -> p (h d)"),
                                ident[:, :]).then_inc(turned, 1)
            pe.wait_ge(att_loaded, N_ATT)

            def body(t, first, last):
                for k in range(K):
                    hidden(t, k)
                    if first and k == 0:
                        turn(0, 1)
                    if k % 2 == 1:
                        u = (k + 1) // 2 + 1
                        if u < U:
                            turn(t, u)
                        elif not last:
                            turn(t + 1, u - U)
                    elif k > 0:
                        scores(t, k - 2)
                        scores(t, k - 1)
                    elif not first:
                        scores(t - 1, K - 2)
                        scores(t - 1, K - 1)
                    if not first and k in POOL_ROUNDS:
                        pool_batch(t - 1, POOL_ROUNDS.index(k), g_ps)
                    if first and k == K // 2:
                        turn_dx()

            blocks(pe, body)
            scores(T - 1, K - 2)
            scores(T - 1, K - 1)
            keep_warm(WARM_SOFTMAX)
            for q in range(NB):
                pool_batch(T - 1, q, g_ps if q == 0 else z_ps[:, q, :], final=True)
            keep_warm(WARM_NORM)
            for h in range(H):
                pe.wait_ge(feat_n_ready[h], 1)
                for m in range(H1 // 128):
                    nc.tensor.matmul(z_ps[:, 2 * h + m, 0:BH], w1_sb[:, m * 128:(m + 1) * 128],
                                     feat_n[:, h * BH:(h + 1) * BH], start=True, stop=True).then_inc(l1_done[h], 1)
            for h in range(H):
                for m in range(H1 // 128):
                    pe.wait_ge(h1_ready[h][m], 1)
                    mm = nc.tensor.matmul(l2_ps[h][:, 0:BH], w2_sb[:, m, :], h1[:, m, h * BH:(h + 1) * BH],
                                          start=(m == 0), stop=(m == H1 // 128 - 1))
                mm.then_inc(l2_done[h], 1)
            for h in range(H):
                pe.wait_ge(h2_ready[h], 1)
                nc.tensor.matmul(l3_ps[h][0:H3, 0:BH], w3_sb[:, :], h2[:, h * BH:(h + 1) * BH],
                                 start=True, stop=True).then_inc(l3_done[h], 1)
            for h in range(H):
                pe.wait_ge(h3_ready[h], 1)
                nc.tensor.matmul(z_ps[0:1, h, 0:BH], wf_sb[:, :], h3[:, h * BH:(h + 1) * BH],
                                 start=True, stop=True).then_inc(logit_done[h], 1)

        @block.scalar
        def _(act):
            def exponentials(t):
                act.wait_ge(max_step, (t + 1) * 3)
                act.wait_ge(skew_done, t * 2 + 2)
                nc.scalar.activation(expd[:, :], s_ps[:, 0:NPAIR], ACT.Exp, bias=neg_max[:, 2:3], scale=1.0,
                                     accum_out=denom[:, 0:1]).then_inc(exp_done, 1)

            nc.scalar.preload_act_table(ACT.Exp)

            def body(t, first, last):
                if first:
                    act.wait_ge(att_loaded, N_ATT)
                for k in range(K):
                    n = t * K + k
                    if not (first and k < RING):
                        act.wait_ge(scored, n - (RING - 1))
                    for half in range(2):
                        act.wait_ge(z_ready, n * 2 + (half + 1))
                        nc.scalar.activation(hid[:, k % RING, 2 * half:2 * half + 2, :],
                                             z_ps[:, 2 * half:2 * half + 2, 0:NPAIR], ACT.Relu,
                                             bias=att_bias[:, :], scale=1.0).then_inc(hid_ready, 1)
                        if not first and k == 1 and half == 0:
                            exponentials(t - 1)

            blocks(act, body)
            exponentials(T - 1)
            spread_diagonal(act, C - 1, nc.scalar.copy)
            act.wait_ge(bn_step, 1)
            nc.scalar.activation(bn_tmp[:, 0:1], bn_mv[:, 1:2], ACT.Sqrt, bias=eps_sb[:, :], scale=1.0).then_inc(std_done, 1)
            nc.scalar.preload_act_table(ACT.Sigmoid)
            act.wait_ge(bn_step, 4)
            nc.scalar.activation(feat_n[:, BH:B], feat[:, BH:B], ACT.Identity, bias=bn_tmp[:, 4:5],
                                 scale=bn_tmp[:, 2:3]).then_inc(feat_n_ready[1], 1)

            def relu_bias(dst, src, bias, ready):
                nc.scalar.activation(dst, src, ACT.Relu, bias=bias, scale=1.0).then_inc(ready, 1)

            for h in range(H):
                act.wait_ge(l1_done[h], 1)
                relu_bias(h1[:, 0, h * BH:(h + 1) * BH], z_ps[:, 2 * h, 0:BH], b1_sb[:, 0:1], h1_ready[h][0])
            act.wait_ge(l2_done[1], 1)
            relu_bias(h2[:, BH:B], l2_ps[1][:, 0:BH], b2_sb[:, :], h2_ready[1])
            act.wait_ge(l3_done[1], 1)
            relu_bias(h3[:, BH:B], l3_ps[1][0:H3, 0:BH], b3_sb[:, :], h3_ready[1])
            for h in range(H):
                act.wait_ge(logit_done[h], 1)
                nc.scalar.activation(prob[:, :].rearrange("a (n h c) -> a h n c", h=H, c=C)[:, h],
                                     z_ps[0:1, h, 0:BH].rearrange("a (n c) -> a n c", c=C), ACT.Sigmoid,
                                     bias=bf_sb[:, :], scale=1.0).then_inc(prob_ready, 1)

        @block.vector
        def _(dve):
            for i, credited in enumerate((g_used, skew_done, pooled_done)):
                nc.vector.memset(credit[:, i:i + 1], 0.0).then_inc(credited, 2)
            for tile in (att_w_diag[:, :], att_d_slide[:, :], dx_rows[:, :, 0:D], att_skew[:, :, :]):
                nc.vector.memset(tile, 0.0).then_inc(zeros_made, 1)
            dve.wait_ge(sx_loaded, 16)
            dve.wait_ge(consts_made, 1)
            nc.vector.tensor_scalar(sx_wrap[:, :, :], sx_raw[:, :, :], 0.0, float(V), ALU.is_lt, ALU.mult).then_inc(rows_step, 1)
            dve.wait_ge(rows_step, 1)
            nc.vector.tensor_tensor(sx_pos[:, :, :], sx_raw[:, :, :], sx_wrap[:, :, :], ALU.add).then_inc(rows_step, 1)
            dve.wait_ge(rows_step, 2)
            nc.vector.tensor_scalar(sx_clip[:, :, :], sx_pos[:, :, :], 0.0, float(V - 1), ALU.max, ALU.min).then_inc(rows_step, 1)
            dve.wait_ge(rows_step, 3)
            base = field_base[:, :].rearrange("p (a f) -> p a f", a=1)
            nc.vector.tensor_tensor(rows_f[:, :, 0:F], sx_clip[:, :, :], base.broadcast_to([128, C, F]),
                                    ALU.add).then_inc(rows_step, 1)
            nc.vector.tensor_tensor(rows_f[:, :, F:Q], sx_clip[:, :, 0:Q - F],
                                    base[:, :, 0:Q - F].broadcast_to([128, C, Q - F]), ALU.add).then_inc(rows_step, 1)
            dve.wait_ge(rows_turned, 1)
            nc.vector.tensor_copy(rows_now[:, :], x_ps[:, 0:K * H]).then_inc(rows_ready, 1)
            nc.vector.tensor_copy(rows_all[:, :], x_ps[:, 0:128]).then_inc(rows_ready, 1)

            def spread_first():
                dve.wait_ge(first_turned, 1)
                src = x_ps[:, 0:128].rearrange("p (c j) -> p c j", j=Q)
                nc.vector.tensor_copy(emb_t[:, 0, :, 0:Q], src).then_inc(first_emb_t_ready, 1)
                nc.vector.tensor_copy(emb_t[:, 0, :, Q:FW], src[:, :, Q - F:FW - F]).then_inc(first_emb_t_ready, 1)

            def spread(t, u):
                dve.wait_ge(turned, t * U + (u + 1))
                n, lo = (1, 1) if isinstance(t, int) and t * U + u == 0 else (2, 0)
                src = tr_ps[:, lo * 128:2 * 128].rearrange("p (x j) -> p x j", j=Q)
                dst = emb_t[:, bass.ds(t * K + 2 * u + lo, n), :, :].rearrange("p n c j -> p (n c) j")
                nc.vector.tensor_copy(dst[:, :, 0:Q], src).then_inc(emb_t_ready, 1)
                nc.vector.tensor_copy(dst[:, :, Q:FW], src[:, :, Q - F:FW - F]).then_inc(emb_t_ready, 1)

            def products(t, k):
                n = t * K + k
                if isinstance(t, int) and t * K + k == 0:
                    dve.wait_ge(first_emb_t_ready, 2)
                elif k % 2 == 0 or (isinstance(t, int) and t * K + k == 1):
                    dve.wait_ge(emb_t_ready, (t * U + (k // 2 + 1)) * 2)
                if not (isinstance(t, int) and t * K + k < RING):
                    dve.wait_ge(z_ready, (n - (RING - 1)) * 2)
                e = emb_t[:, bass.ds(n, 1), :, :].rearrange("p n c j -> p (n c) j")
                row = list(e.ap)
                part, step_c = row[0], row[1]
                left = bass.AP(e.tensor, e.offset, [part, step_c, [0, NDELTA], [1, F]])
                right = bass.AP(e.tensor, e.offset + 1, [part, step_c, [1, NDELTA], [1, F]])
                slot = prod[:, k % RING, :, :]
                nc.vector.tensor_tensor(slot[:, :, 0:NFULL].rearrange("p c (s i) -> p c s i", i=F), left, right,
                                        ALU.mult).then_inc(prod_ready, 1)
                nc.vector.tensor_tensor(slot[:, :, NFULL:NPAIR], e[:, :, 0:F // 2], e[:, :, F // 2:F],
                                        ALU.mult).then_inc(prod_ready, 1)

            def maxima(t):
                dve.wait_ge(scored, (t + 1) * K)
                nc.vector.reduce_max(neg_max[:, 0:1], s_ps[:, 0:NPAIR], AX.X).then_inc(max_step, 1)
                dve.wait_ge(max_step, t * 3 + 1)
                nc.vector.tensor_tensor(neg_max[:, 1:2], neg_max[:, 0:1], score_bias[:, :], ALU.add).then_inc(max_step, 1)
                dve.wait_ge(max_step, t * 3 + 2)
                nc.vector.tensor_tensor(neg_max[:, 2:3], score_bias[:, :], neg_max[:, 1:2], ALU.subtract).then_inc(max_step, 1)

            def weights(t):
                dve.wait_ge(exp_done, t + 1)
                nc.vector.reciprocal(denom[:, 1:2], denom[:, 0:1]).then_inc(inv_done, 1)
                dve.wait_ge(inv_done, t + 1)
                base = att_skew[:, :, :]
                part = list(base.ap)[0]
                full = bass.AP(base.tensor, base.offset + 1, [part, [1, NDELTA], [FW + 1, F]])
                half = bass.AP(base.tensor, base.offset + F // 2, [part, [FW + 1, F // 2]])
                nc.vector.tensor_scalar(full, expd[:, 0:NFULL].rearrange("p (s i) -> p s i", i=F),
                                        denom[:, 1:2], None, ALU.mult).then_inc(skew_done, 1)
                nc.vector.tensor_scalar(half, expd[:, NFULL:NPAIR], denom[:, 1:2], None, ALU.mult).then_inc(skew_done, 1)
                dve.wait_ge(skew_done, (t + 1) * 2 + 2)
                lo = Q - NDELTA
                nc.vector.tensor_copy(att_skew[:, lo:F, Q - F:FW - F], att_skew[:, lo:F, Q:FW]).then_inc(fold_done, 1)

            def diagonal(t, c):
                if c == 0:
                    dve.wait_ge(fold_done, t + 1)
                    dve.wait_ge(g_used, t * NB + 2)
                quad = slice(Q * c, Q * (c + 1))
                nc.vector.transpose(att_diag[quad, :, c, :].rearrange("p m i -> p i m"),
                                    att_skew[quad, :, 0:Q]).then_inc(diag_ready, 1)

            def pooling(t, q, bank):
                dve.wait_ge(g_ready, t * NB + (q + 1))
                dve.wait_ge(pooled_done, t * NB + (q + 1))
                e = emb_t[:, bass.ds(t * K + q * KB, KB), :, 0:F].rearrange("p n c j -> p (n c) j")
                nc.vector.tensor_tensor(pooled_i[:, q % 2, :, :], bank[:, 0:KB * C * F].rearrange("p (x i) -> p x i", i=F), e,
                                        ALU.mult).then_inc(g_used, 1)
                dve.wait_ge(g_used, t * NB + (q + 3))
                nc.vector.tensor_reduce(pooled[:, bass.ds(t * (K * C) + q * (KB * C), KB * C)], pooled_i[:, q % 2, :, :],
                                        AX.X, ALU.add).then_inc(pooled_done, 1)

            def statistics(t):
                dve.wait_ge(pooled_done, (t + 1) * NB + 2)
                cols = bass.ds(t * (K * C), K * C)
                for h in range(H):
                    nc.vector.tensor_copy(feat_h[0:D, h, cols], pooled[h * D:(h + 1) * D, cols]).then_inc(feat_ready, 1)
                dve.wait_ge(feat_ready, (t + 1) * H + 2)
                for h in range(H):
                    last = nc.vector.bn_stats(bn_raw[:, bass.ds(t * H + h, 1), :].rearrange("p a s -> p (a s)"), feat_h[:, h, cols])
                    last.then_inc(stats_done, 1)

            feat_h = feat[:, :].rearrange("p (h n) -> p h n", h=H)

            def body(t, first, last):
                for k in range(K):
                    if first and k < 2:
                        spread_first() if k == 0 else spread(t, 0)
                    elif k % 2 == 0:
                        spread(t, k // 2)
                    products(t, k)
                    if first:
                        if k == K // 2:
                            nc.vector.memset(att_diag[:, :, :, :], 0.0).then_inc(zeros_made, 1)
                        elif k == K // 2 + 2:
                            dve.wait_ge(dx_turned, 1)
                            nc.vector.tensor_copy(feat[D:FEA, :].rearrange("p (h n c) -> p h n c", h=H, c=C),
                                                  x_ps[D:FEA, :].rearrange("p (n h c) -> p h n c", h=H, c=C)).then_inc(feat_ready, 2)
                        continue
                    if k == 3:
                        maxima(t - 1)
                        weights(t - 1)
                    elif k in (4, 5):
                        diagonal(t - 1, 2 * (k - 4))
                        diagonal(t - 1, 2 * (k - 4) + 1)
                    elif k - 2 in POOL_ROUNDS:
                        pooling(t - 1, POOL_ROUNDS.index(k - 2), g_ps)
                        if k - 2 == POOL_ROUNDS[-1]:
                            statistics(t - 1)

            blocks(dve, body)
            maxima(T - 1)
            weights(T - 1)
            dve.wait_ge(fold_done, T)
            dve.wait_ge(g_used, (T - 1) * NB + 2)
            nc.vector.transpose(att_compact[:, :, :], att_skew[:, :, 0:Q]).then_inc(compact_ready, 1)
            for c in range(C - 2):
                spread_diagonal(dve, c, nc.vector.tensor_copy)
            for q in range(NB):
                pooling(T - 1, q, g_ps if q == 0 else z_ps[:, q, :])
            statistics(T - 1)
            dve.wait_ge(stats_done, T * H)
            nc.vector.bn_aggr(bn_mv[:, :], bn_raw[:, :, :].rearrange("p t s -> p (t s)")).then_inc(bn_step, 1)
            dve.wait_ge(std_done, 1)
            dve.wait_ge(dense_loaded, N_DENSE)
            nc.vector.reciprocal(bn_tmp[:, 1:2], bn_tmp[:, 0:1]).then_inc(bn_step, 1)
            dve.wait_ge(bn_step, 2)
            nc.vector.tensor_tensor(bn_tmp[:, 2:3], bn_tmp[:, 1:2], gamma_sb[:, :], ALU.mult).then_inc(bn_step, 1)
            nc.vector.tensor_scalar(bn_tmp[:, 3:4], bn_mv[:, 0:1], -1.0, None, ALU.mult).then_inc(neg_mean, 1)
            dve.wait_ge(neg_mean, 1)
            dve.wait_ge(bn_step, 3)
            nc.vector.scalar_tensor_tensor(out=bn_tmp[:, 4:5], in0=bn_tmp[:, 2:3], scalar=bn_tmp[:, 3:4],
                                           in1=beta_sb[:, :], op0=ALU.mult, op1=ALU.add).then_inc(bn_step, 1)
            dve.wait_ge(bn_step, 4)
            nc.vector.tensor_scalar(feat_n[:, 0:BH], feat[:, 0:BH], bn_tmp[:, 2:3], bn_tmp[:, 4:5], ALU.mult,
                                    ALU.add).then_inc(feat_n_ready[0], 1)

            def relu_bias(dst, src, bias, ready):
                nc.vector.tensor_scalar(dst, src, bias, 0.0, ALU.add, ALU.max).then_inc(ready, 1)

            for h in range(H):
                dve.wait_ge(l1_done[h], 2)
                relu_bias(h1[:, 1, h * BH:(h + 1) * BH], z_ps[:, 2 * h + 1, 0:BH], b1_sb[:, 1:2], h1_ready[h][1])
            dve.wait_ge(l2_done[0], 1)
            relu_bias(h2[:, 0:BH], l2_ps[0][:, 0:BH], b2_sb[:, :], h2_ready[0])
            dve.wait_ge(l3_done[0], 1)
            relu_bias(h3[:, 0:BH], l3_ps[0][0:H3, 0:BH], b3_sb[:, :], h3_ready[0])


_INS = ['r_dx', 'r_sx', 'L0_rec_emb_table', 'L0_rec_att_w_W', 'L0_rec_att_w_b', 'L0_rec_att_d_W',
        'L0_rec_att_d_b', 'L0_rec_bn_gamma', 'L0_rec_bn_beta', 'L0_rec_w1', 'L0_rec_b1', 'L0_rec_w2',
        'L0_rec_b2', 'L0_rec_w3', 'L0_rec_b3', 'L0_rec_wf', 'L0_rec_bf']


def kernel(**inputs):
    import numpy as np
    import concourse.bacc as bacc
    from concourse.bass_utils import run_bass_kernel_spmd

    nc = bacc.Bacc("TRN2", target_bir_lowering=False, num_devices=1)
    arrays, args = {}, []
    for name in _INS:
        a = np.ascontiguousarray(inputs[name])
        arrays[f"in_{name}"] = a
        args.append(nc.dram_tensor(f"in_{name}", a.shape, mybir.dt.from_np(a.dtype), kind="ExternalInput").ap())
    args.append(nc.dram_tensor("out_prob", (B,), F32, kind="ExternalOutput").ap())
    afm_kernel(nc, *args)
    r = run_bass_kernel_spmd(nc, [arrays], core_ids=[0])
    return r.results[0]["out_prob"]
```

```python
import concourse.bass as bass
from concourse import mybir
from contextlib import ExitStack

F32 = mybir.dt.float32
F32R = mybir.dt.float32r
I32 = mybir.dt.int32
ALU = mybir.AluOpType
ACT = mybir.ActivationFunctionType
AX = mybir.AxisListType

B, F, V, D, A, ND = 512, 26, 12500, 64, 64, 13
H1, H2, H3 = 256, 128, 64
FEA = D + ND
EPS = 1e-5
H, C, K, T = 2, 4, 16, 4
BH = B // H
Q = 32
NDELTA = F // 2 - 1
NFULL = NDELTA * F
NPAIR = F * (F - 1) // 2
FW = F + NDELTA
U = K // 2
OPENING = 2
PROD_RING, RING = 8, 4
NB = 4
KB = K // NB
SPLIT = (1, 5, 7, 9, 11, 13, 15)
SPLIT_FROM = 9
NP2 = NPAIR + NPAIR % 2
assert T * K * H * C == B and C * Q == 128 and H * D == 128 and NFULL + F // 2 == NPAIR


def afm_kernel(nc, dx, sx, table, att_w, att_wb, att_d, att_db, gamma, beta,
               w1, b1, w2, b2, w3, b3, wf, bf, out):
    with ExitStack() as ctx:
        def sb(name, shape, dt=F32):
            return ctx.enter_context(nc.sbuf_tensor(name, shape, dt))

        def ps(name, shape):
            return ctx.enter_context(nc.psum_tensor(name, shape, F32))

        def sem(name):
            return ctx.enter_context(nc.semaphore(name))

        ident = sb("ident", [128, 128])
        att_w_diag = sb("att_w_diag", [128, 128])
        att_bias = sb("att_bias", [128, 1])
        att_d_slide = sb("att_d_slide", [128, 2 * (K - 1) + Q])
        score_bias = sb("score_bias", [128, 1])
        w1_sb = sb("w1_sb", [FEA, H1])
        w2_sb = sb("w2_sb", [128, H1 // 128, H2])
        w3_sb = sb("w3_sb", [H2, H3])
        wf_sb = sb("wf_sb", [H3, 1])
        b1_sb = sb("b1_sb", [128, H1 // 128])
        b2_sb = sb("b2_sb", [H2, 1])
        b3_sb = sb("b3_sb", [H3, 1])
        bf_sb = sb("bf_sb", [1, 1])
        gamma_sb = sb("gamma_sb", [FEA, 1])
        beta_sb = sb("beta_sb", [FEA, 1])
        eps_sb = sb("eps_sb", [FEA, 1])
        dx_rows = sb("dx_rows", [128, T, FEA])

        sx_raw = sb("sx_raw", [128, C, F], I32)
        field_base = sb("field_base", [128, F], I32)
        sx_wrap = sb("sx_wrap", [128, C, F])
        sx_pos = sb("sx_pos", [128, C, F])
        sx_clip = sb("sx_clip", [128, C, F])
        rows_f = sb("rows_f", [128, C, Q])
        rows_all = sb("rows_all", [128, 128], I32)
        rows_now = sb("rows_now", [128, K * H], I32)

        emb = sb("emb", [128, K, H, D])
        emb_keep = sb("emb_keep", [128, K, H, D])
        emb_t = sb("emb_t", [128, T * K, C, FW])
        prod = sb("prod", [128, PROD_RING, C, NPAIR])
        hid = sb("hid", [128, RING, C, NPAIR])
        att_w_high = sb("att_w_high", [128, 128], F32R)
        att_w_low = sb("att_w_low", [128, 128], F32R)
        prod_high = sb("prod_high", [128, RING, C, NP2], F32R)
        prod_low = sb("prod_low", [128, RING, C, NP2], F32R)
        neg_max = sb("neg_max", [128, 2])
        expd = sb("expd", [128, NPAIR])
        denom = sb("denom", [128, 2])
        att_skew = sb("att_skew", [128, F, FW])
        att_compact = sb("att_compact", [128, F, Q])
        att_diag = sb("att_diag", [128, Q, C, F])
        pooled_i = sb("pooled_i", [128, 2, KB * C, F])
        pooled = sb("pooled", [128, T * K * C])

        feat = sb("feat", [FEA, B])
        bn_raw = sb("bn_raw", [FEA, T * H, 6])
        bn_mv = sb("bn_mv", [FEA, 2])
        bn_tmp = sb("bn_tmp", [FEA, 5])
        feat_n = sb("feat_n", [FEA, B])
        h1 = sb("h1", [128, H1 // 128, B])
        h2 = sb("h2", [H2, B])
        h3 = sb("h3", [H3, B])
        prob = sb("prob", [1, B])

        credit = sb("credit", [1, 4])
        z_ps = ps("z_ps", [128, C, 512])
        s_ps = ps("s_ps", [128, 512])
        tr_ps = ps("tr_ps", [128, 512])
        g_ps = ps("g_ps", [128, 512])
        x_ps = ps("x_ps", [128, 512])
        l2_ps, l3_ps = (g_ps, tr_ps), (x_ps, s_ps)

        sx_loaded = sem("sx_loaded")
        consts_made = sem("consts_made")
        zeros_made = sem("zeros_made")
        att_loaded = sem("att_loaded")
        dense_loaded = sem("dense_loaded")
        rows_step = sem("rows_step")
        rows_turned = sem("rows_turned")
        rows_ready = sem("rows_ready")
        rows_here = sem("rows_here")
        gathered = [sem(f"gathered{u}") for u in range(U)]
        kept = [sem(f"kept{u}") for u in range(U)]
        first_gathered = [sem(f"first_gathered{u}") for u in range(OPENING)]
        first_turned = sem("first_turned")
        first_emb_t_ready = sem("first_emb_t_ready")
        turned = sem("turned")
        emb_t_ready = sem("emb_t_ready")
        prod_ready = sem("prod_ready")
        w_split = sem("w_split")
        high_ready = sem("high_ready")
        low_ready = sem("low_ready")
        z_ready = sem("z_ready")
        hid_ready = sem("hid_ready")
        scored = sem("scored")
        max_step = sem("max_step")
        exp_done = sem("exp_done")
        inv_done = sem("inv_done")
        skew_done = sem("skew_done")
        fold_done = sem("fold_done")
        diag_ready = sem("diag_ready")
        compact_ready = sem("compact_ready")
        spread_ready = sem("spread_ready")
        g_ready = sem("g_ready")
        g_used = sem("g_used")
        pooled_done = sem("pooled_done")
        dx_turned = sem("dx_turned")
        feat_ready = sem("feat_ready")
        stats_done = sem("stats_done")
        bn_step = sem("bn_step")
        neg_mean = sem("neg_mean")
        std_done = sem("std_done")
        feat_n_ready = [sem(f"feat_n_ready{h}") for h in range(H)]
        l1_done = [sem(f"l1_done{h}") for h in range(H)]
        h1_ready = [[sem(f"h1_ready{h}{m}") for m in range(H1 // 128)] for h in range(H)]
        l2_done = [sem(f"l2_done{h}") for h in range(H)]
        h2_ready = [sem(f"h2_ready{h}") for h in range(H)]
        l3_done = [sem(f"l3_done{h}") for h in range(H)]
        h3_ready = [sem(f"h3_ready{h}") for h in range(H)]
        logit_done = [sem(f"logit_done{h}") for h in range(H)]
        prob_ready = sem("prob_ready")
        stored = sem("stored")
        POOL_ROUNDS, LAST_POOL_ROUNDS, OWN_POOL_ROUNDS = [4, 6, 8, 10], [4, 5, 6, 7], [15]
        PART_ROUNDS = K // 2
        PART_BATCHES = NB // 2
        HIGH_HALF = (0, 1)
        MAX_AT, POOL_LATER, LOW_LATER = 3, 4, 2
        DIAG_ROUNDS, OWN_DIAG_ROUNDS = [2, 3], [12, 13]
        OWN_EXP, OWN_MAX = 2, 4
        WARM_GATHER, WARM_PRODUCT, WARM_SOFTMAX, WARM_NORM = 10, 5, 16, 18
        N_ATT, N_DENSE = 16 * 7, 16 * 13

        TURNS = {2 * u - 5: u for u in range(3, U + 3)}
        FIRST_TURNS = {2: 2, 4: 3, 5: 4, 6: 5, 8: 6, 9: 7, 11: 8, 13: 9, 15: 10}

        def to_turn(k, first, last):
            unit = (FIRST_TURNS if first else TURNS).get(k)
            return None if unit is None or (last and unit >= U) else divmod(unit, U)

        def is_split(t, k):
            return k in SPLIT and not (isinstance(t, int) and t == 0 and k < SPLIT_FROM)

        def split_count(t, k):
            unsplit = sum(1 for early in SPLIT if early < SPLIT_FROM)
            return t * len(SPLIT) + (SPLIT.index(k) + 1 - unsplit)

        def landed(t, u):
            return (t + 1) * 64 - 32 if u < OPENING else (t + 1) * 64

        def blocks(engine, body):
            body(0, True, False)
            with engine.Fori(1, T - 1) as t:
                body(t, False, False)
            body(T - 1, False, True)

        def spread_diagonal(engine, c, copy):
            engine.wait_ge(compact_ready, T + 1)
            quad, rows = slice(Q * c, Q * (c + 1)), slice(PART_ROUNDS * H, Q)
            copy(att_diag[quad, rows, c, :].rearrange("p m i -> p i m"),
                 att_compact[quad, :, rows]).then_inc(spread_ready, 1)

        block = ctx.enter_context(nc.Block())

        @block.sync
        def _(sp):
            sp.dma_start(sx_raw[:, :, :], sx.rearrange("(g c) f -> g c f", c=C)).then_inc(sx_loaded, 16)
            sp.wait_ge(zeros_made, 2)
            for h in range(H):
                p = h * D
                sp.dma_start(att_w_diag[p:p + D, h * A:(h + 1) * A], att_w).then_inc(att_loaded, 16)
                sp.dma_start(att_d_slide[p:p + D, 2 * (K - 1) + h:2 * (K - 1) + h + 1],
                             att_d).then_inc(att_loaded, 16)
                sp.dma_start(att_bias[p:p + D, :], att_wb.rearrange("(a n) -> a n", n=1)).then_inc(att_loaded, 16)
            sp.dma_start(score_bias[:, :], att_db.partition_broadcast(128)).then_inc(att_loaded, 16)
            sp.dma_start(w1_sb[:, :], w1).then_inc(dense_loaded, 16)
            sp.dma_start(w2_sb[:, :, :], w2.rearrange("(m p) n -> p m n", p=128)).then_inc(dense_loaded, 16)
            sp.dma_start(w3_sb[:, :], w3).then_inc(dense_loaded, 16)
            sp.dma_start(wf_sb[:, :], wf).then_inc(dense_loaded, 16)
            for m in range(H1 // 128):
                sp.dma_start(b1_sb[:, m:m + 1],
                             b1[m * 128:(m + 1) * 128].rearrange("(p n) -> p n", n=1)).then_inc(dense_loaded, 16)
            sp.dma_start(b2_sb[:, :], b2.rearrange("(p n) -> p n", n=1)).then_inc(dense_loaded, 16)
            sp.dma_start(b3_sb[:, :], b3.rearrange("(p n) -> p n", n=1)).then_inc(dense_loaded, 16)
            sp.dma_start(bf_sb[:, :], bf.rearrange("(p n) -> p n", n=1)).then_inc(dense_loaded, 16)
            sp.dma_start(gamma_sb[:, :], gamma.rearrange("(p n) -> p n", n=1)).then_inc(dense_loaded, 16)
            sp.dma_start(beta_sb[:, :], beta.rearrange("(p n) -> p n", n=1)).then_inc(dense_loaded, 16)
            sp.wait_ge(zeros_made, 3)
            for hh in range(2):
                sp.dma_start(dx_rows[:, 2 * hh:2 * hh + 2, D:FEA],
                             dx.rearrange("(t p) n -> p t n", p=128)[:, 2 * hh:2 * hh + 2, :]).then_inc(dense_loaded, 16)

            def body(t, first, last):
                for u in range(U):
                    if first:
                        sp.wait_ge(turned, u + 1)
                    else:
                        sp.wait_ge(g_ready, (t - 1) * NB + (u // (U // NB) + 1))
                    if last:
                        sp.wait_ge(turned, t * U + (u + 1))
                    sp.dma_start(emb_keep[:, 2 * u:2 * u + 2, :, :],
                                 emb[:, 2 * u:2 * u + 2, :, :]).then_inc(kept[u], 16)

            blocks(sp, body)
            sp.wait_ge(prob_ready, H)
            sp.dma_start(out.rearrange("(a n) -> a n", a=1), prob[:, :]).then_inc(stored, 16)
            sp.wait_ge(stored, 16)

        @block.gpsimd
        def _(pool):
            nc.gpsimd.iota(field_base[:, :], pattern=[[V, F]], base=0, channel_multiplier=0).then_inc(consts_made, 1)
            nc.gpsimd.memset(ident[:, :], 0.0).then_inc(consts_made, 1)
            nc.gpsimd.memset(eps_sb[:, :], EPS).then_inc(consts_made, 1)
            pool.wait_ge(consts_made, 3)
            nc.gpsimd.affine_select(out=ident[:, :], in_=ident[:, :], compare_op=ALU.not_equal, fill=1.0,
                                    base=0, pattern=[[-1, 128]], channel_multiplier=1).then_inc(consts_made, 1)

            def body(t, first, last):
                if first:
                    pool.wait_ge(rows_ready, 1)
                else:
                    for u in range(U):
                        pool.wait_ge(gathered[u], landed(t - 1, u))
                    pool.wait_ge(rows_ready, 2)
                    pool.wait_ge(kept[0], t * 16)
                    nc.gpsimd.tensor_copy(rows_now[:, :], rows_all[:, bass.ds(t * (K * H), K * H)]).then_inc(rows_here, 16)
                    pool.wait_ge(rows_ready, 2)
                    pool.wait_ge(rows_here, t * 16)
                for k in range(K):
                    u = k // 2
                    if not first and k % 2 == 0 and k > 0:
                        pool.wait_ge(rows_ready, 2)
                        pool.wait_ge(kept[u], t * 16)
                    for h in range(H):
                        nc.gpsimd.indirect_dma_start(
                            emb[:, k, h, :], None, table.rearrange("f v d -> (f v) d"),
                            bass.IndirectOffsetOnAxis(ap=rows_now[:, k * H + h:k * H + h + 1], axis=0),
                        ).then_inc(first_gathered[u] if first and k % 2 == 0 and u < OPENING else gathered[u], 16)

            blocks(pool, body)

        @block.tensor
        def _(pe):
            def turn(t, u):
                pe.wait_ge(gathered[u], landed(t, u))
                pe.wait_ge(emb_t_ready, (t * U + u) * 2)
                for j in range(2):
                    last = nc.tensor.transpose(tr_ps[:, j * 128:(j + 1) * 128],
                                               emb[:, 2 * u + j, :, :].rearrange("p h d -> p (h d)"), ident[:, :])
                last.then_inc(turned, 1)

            def turn_first(u):
                pe.wait_ge(first_gathered[u], 32)
                if u > 0:
                    pe.wait_ge(first_emb_t_ready, u * 2)
                nc.tensor.transpose(x_ps[:, 0:128], emb[:, 2 * u, :, :].rearrange("p h d -> p (h d)"),
                                    ident[:, :]).then_inc(first_turned, 1)

            def turn_second(u):
                pe.wait_ge(gathered[u], landed(0, u))
                if u > 0:
                    pe.wait_ge(emb_t_ready, u * 2)
                nc.tensor.transpose(tr_ps[:, 128:256], emb[:, 2 * u + 1, :, :].rearrange("p h d -> p (h d)"),
                                    ident[:, :]).then_inc(turned, 1)

            def hidden(t, k):
                n = t * K + k
                if is_split(t, k):
                    pe.wait_ge(low_ready, split_count(t, k))
                else:
                    pe.wait_ge(prod_ready, (n + 1) * 2)
                for c in range(C):
                    if c % 2 == 0 and not (isinstance(t, int) and t * K + k == 0):
                        pe.wait_ge(hid_ready, n * 2 + (c // 2 - 1))
                    if is_split(t, k):
                        high, low = prod_high[:, k % RING, c, :], prod_low[:, k % RING, c, :]
                        nc.tensor.matmul(z_ps[:, c, 0:NP2], att_w_low[:, :], high, start=True, stop=False)
                        nc.tensor.matmul(z_ps[:, c, 0:NP2], att_w_high[:, :], low, start=False, stop=False)
                        mm = nc.tensor.matmul(z_ps[:, c, 0:NP2], att_w_high[:, :], high, start=False, stop=True)
                    else:
                        mm = nc.tensor.matmul(z_ps[:, c, 0:NPAIR], att_w_diag[:, :], prod[:, k % PROD_RING, c, 0:NPAIR],
                                              start=True, stop=True)
                    if c % 2 == 1:
                        mm.then_inc(z_ready, 1)

            def scores(t, k):
                n = t * K + k
                pe.wait_ge(hid_ready, (n + 1) * 2)
                if k == 0 and not (isinstance(t, int) and t == 0):
                    pe.wait_ge(exp_done, t)
                parts = isinstance(t, int) and t == T - 1
                if parts and k == PART_ROUNDS:
                    pe.wait_ge(feat_ready, 2)
                for c in range(C):
                    mm = nc.tensor.matmul((x_ps if parts and k >= PART_ROUNDS else s_ps)[Q * c:Q * (c + 1), 0:NPAIR],
                                          att_d_slide[:, 2 * (K - 1 - k):2 * (K - 1 - k) + Q],
                                          hid[:, k % RING, c, :],
                                          start=(k == 0 or (parts and k == PART_ROUNDS)),
                                          stop=(k == K - 1 or (parts and k == PART_ROUNDS - 1)))
                mm.then_inc(scored, 1)

            def pool_batch(t, q, bank):
                if bank is not g_ps:
                    pe.wait_ge(spread_ready, C)
                elif q == 0:
                    pe.wait_ge(diag_ready, (t + 1) * C + 2)
                for u in range(q * (U // NB), (q + 1) * (U // NB)):
                    pe.wait_ge(kept[u], (t + 1) * 16)
                if bank is g_ps:
                    pe.wait_ge(g_used, t * NB + (q + 2))
                for j in range(KB):
                    k = q * KB + j
                    for h in range(H):
                        mm = nc.tensor.matmul(bank[D * h:D * (h + 1), j * C * F:(j + 1) * C * F],
                                              emb_keep[:, k, h, :],
                                              att_diag[:, k * H + h, :, :].rearrange("p c i -> p (c i)"),
                                              start=True, stop=True)
                mm.then_inc(g_ready, 1)

            def turn_dx():
                pe.wait_ge(dense_loaded, N_DENSE)
                pe.wait_ge(first_emb_t_ready, OPENING * 2)
                for t in range(T):
                    mm = nc.tensor.transpose(x_ps[0:FEA, t * 128:(t + 1) * 128], dx_rows[:, t, :], ident[:, :])
                mm.then_inc(dx_turned, 1)

            def keep_warm(n, bank):
                for _ in range(n):
                    nc.tensor.matmul(bank[:, 0:128], ident[:, :], ident[:, :], start=True, stop=True)

            pe.wait_ge(consts_made, 4)
            pe.wait_ge(rows_step, 5)
            nc.tensor.transpose(x_ps[:, 0:128], rows_f[:, :, :].rearrange("p c j -> p (c j)"),
                                ident[:, :]).then_inc(rows_turned, 1)
            keep_warm(WARM_GATHER, g_ps)
            pe.wait_ge(rows_ready, 2)
            turn_first(0)
            keep_warm(WARM_PRODUCT, g_ps)
            turn_second(0)
            pe.wait_ge(att_loaded, N_ATT)

            def body(t, first, last):
                for k in range(K):
                    hidden(t, k)
                    if first and k in (0, 1):
                        turn_first(1) if k == 0 else turn_second(1)
                    if k % 2 == 0 and k > 0:
                        scores(t, k - 2)
                        scores(t, k - 1)
                    elif k == 0 and not first:
                        scores(t - 1, K - 2)
                        scores(t - 1, K - 1)
                    unit = to_turn(k, first, last)
                    if unit:
                        turn(t + unit[0], unit[1])
                    pool_rounds = LAST_POOL_ROUNDS if last else POOL_ROUNDS
                    if not first and k in pool_rounds:
                        pool_batch(t - 1, pool_rounds.index(k), g_ps)
                    if last and k in OWN_POOL_ROUNDS:
                        pool_batch(t, OWN_POOL_ROUNDS.index(k), g_ps)
                    if first and k == K // 2 - 2:
                        turn_dx()

            blocks(pe, body)
            scores(T - 1, K - 2)
            scores(T - 1, K - 1)
            pe.wait_ge(emb_t_ready, T * U * 2)
            for q in range(len(OWN_POOL_ROUNDS), PART_BATCHES):
                pool_batch(T - 1, q, g_ps)
            keep_warm(WARM_SOFTMAX, tr_ps)
            for q in range(PART_BATCHES, NB):
                pool_batch(T - 1, q, z_ps[:, q, :])
            keep_warm(WARM_NORM, tr_ps)
            for h in range(H):
                pe.wait_ge(feat_n_ready[h], 1)
                for m in range(H1 // 128):
                    nc.tensor.matmul(z_ps[:, 2 * h + m, 0:BH], w1_sb[:, m * 128:(m + 1) * 128],
                                     feat_n[:, h * BH:(h + 1) * BH], start=True, stop=True).then_inc(l1_done[h], 1)
            for h in range(H):
                for m in range(H1 // 128):
                    pe.wait_ge(h1_ready[h][m], 1)
                    mm = nc.tensor.matmul(l2_ps[h][:, 0:BH], w2_sb[:, m, :], h1[:, m, h * BH:(h + 1) * BH],
                                          start=(m == 0), stop=(m == H1 // 128 - 1))
                mm.then_inc(l2_done[h], 1)
            for h in range(H):
                pe.wait_ge(h2_ready[h], 1)
                nc.tensor.matmul(l3_ps[h][0:H3, 0:BH], w3_sb[:, :], h2[:, h * BH:(h + 1) * BH],
                                 start=True, stop=True).then_inc(l3_done[h], 1)
            for h in range(H):
                pe.wait_ge(h3_ready[h], 1)
                nc.tensor.matmul(z_ps[0:1, h, 0:BH], wf_sb[:, :], h3[:, h * BH:(h + 1) * BH],
                                 start=True, stop=True).then_inc(logit_done[h], 1)

        @block.scalar
        def _(act):
            def exponentials(s, bank):
                act.wait_ge(max_step, (s + 1) * 2)
                act.wait_ge(skew_done, s * 2 + 2)
                nc.scalar.activation(expd[:, :], bank[:, 0:NPAIR], ACT.Exp, bias=neg_max[:, 1:2], scale=1.0,
                                     accum_out=denom[:, 0:1]).then_inc(exp_done, 1)

            def spread(t, u):
                act.wait_ge(turned, t * U + (u + 1))
                src = tr_ps[:, 0:2 * 128].rearrange("p (x j) -> p x j", j=Q)
                dst = emb_t[:, bass.ds(t * K + 2 * u, 2), :, :].rearrange("p n c j -> p (n c) j")
                nc.scalar.copy(dst[:, :, 0:Q], src).then_inc(emb_t_ready, 1)
                nc.scalar.copy(dst[:, :, Q:FW], src[:, :, Q - F:FW - F]).then_inc(emb_t_ready, 1)

            def diagonal(s, c):
                if c == 0:
                    act.wait_ge(compact_ready, s + 1)
                    act.wait_ge(g_used, s * NB + 2)
                quad = slice(Q * c, Q * (c + 1))
                nc.scalar.copy(att_diag[quad, :, c, :].rearrange("p m i -> p i m"),
                               att_compact[quad, :, :]).then_inc(diag_ready, 1)

            def high_part(t, k):
                act.wait_ge(prod_ready, (t * K + (k + 1)) * 2)
                nc.scalar.copy(prod_high[:, k % RING, :, 0:NPAIR], prod[:, k % PROD_RING, :, 0:NPAIR]).then_inc(high_ready, 1)

            nc.scalar.preload_act_table(ACT.Exp)

            def body(t, first, last):
                if first:
                    act.wait_ge(att_loaded, N_ATT)
                for k in range(K):
                    n = t * K + k
                    if not (first and k < RING):
                        act.wait_ge(scored, n - (RING - 1))
                    for half in range(2):
                        act.wait_ge(z_ready, n * 2 + (half + 1))
                        nc.scalar.activation(hid[:, k % RING, 2 * half:2 * half + 2, :],
                                             z_ps[:, 2 * half:2 * half + 2, 0:NPAIR], ACT.Relu,
                                             bias=att_bias[:, :], scale=1.0).then_inc(hid_ready, 1)
                        if not first and k == 1 and half == 0:
                            exponentials(t - 1, s_ps)
                        if last and k == PART_ROUNDS + OWN_EXP and half == 0:
                            exponentials(t, s_ps)
                        ahead = divmod(k + 2, K)
                        if half == (0 if last and k + 3 == K else HIGH_HALF[k % 2]) and not (last and ahead[0]) and is_split(t + ahead[0], ahead[1]):
                            high_part(t + ahead[0], ahead[1])
                    for i in range(2):
                        if not first and k in DIAG_ROUNDS:
                            diagonal(t - 1, DIAG_ROUNDS.index(k) * 2 + i)
                        if last and k in OWN_DIAG_ROUNDS:
                            diagonal(t, OWN_DIAG_ROUNDS.index(k) * 2 + i)
                    unit = to_turn(k, first, last)
                    if unit:
                        spread(t + unit[0], unit[1])

            blocks(act, body)
            exponentials(T, x_ps)
            spread_diagonal(act, C - 1, nc.scalar.copy)
            act.wait_ge(bn_step, 1)
            nc.scalar.activation(bn_tmp[:, 0:1], bn_mv[:, 1:2], ACT.Sqrt, bias=eps_sb[:, :], scale=1.0).then_inc(std_done, 1)
            nc.scalar.preload_act_table(ACT.Sigmoid)
            def relu_bias(dst, src, bias, ready):
                nc.scalar.activation(dst, src, ACT.Relu, bias=bias, scale=1.0).then_inc(ready, 1)

            for h in range(H):
                act.wait_ge(l1_done[h], 1)
                relu_bias(h1[:, 0, h * BH:(h + 1) * BH], z_ps[:, 2 * h, 0:BH], b1_sb[:, 0:1], h1_ready[h][0])
            act.wait_ge(l2_done[1], 1)
            relu_bias(h2[:, BH:B], l2_ps[1][:, 0:BH], b2_sb[:, :], h2_ready[1])
            act.wait_ge(l3_done[1], 1)
            relu_bias(h3[:, BH:B], l3_ps[1][0:H3, 0:BH], b3_sb[:, :], h3_ready[1])
            for h in range(H):
                act.wait_ge(logit_done[h], 1)
                nc.scalar.activation(prob[:, :].rearrange("a (n h c) -> a h n c", h=H, c=C)[:, h],
                                     z_ps[0:1, h, 0:BH].rearrange("a (n c) -> a n c", c=C), ACT.Sigmoid,
                                     bias=bf_sb[:, :], scale=1.0).then_inc(prob_ready, 1)

        @block.vector
        def _(dve):
            for i, credited in enumerate((g_used, skew_done, pooled_done, diag_ready)):
                nc.vector.memset(credit[:, i:i + 1], 0.0).then_inc(credited, 2)
            for tile in (att_w_diag[:, :], att_d_slide[:, :], dx_rows[:, :, 0:D], att_skew[:, :, :]):
                nc.vector.memset(tile, 0.0).then_inc(zeros_made, 1)
            dve.wait_ge(sx_loaded, 16)
            dve.wait_ge(consts_made, 1)
            nc.vector.tensor_scalar(sx_wrap[:, :, :], sx_raw[:, :, :], 0.0, float(V), ALU.is_lt, ALU.mult).then_inc(rows_step, 1)
            dve.wait_ge(rows_step, 1)
            nc.vector.tensor_tensor(sx_pos[:, :, :], sx_raw[:, :, :], sx_wrap[:, :, :], ALU.add).then_inc(rows_step, 1)
            dve.wait_ge(rows_step, 2)
            nc.vector.tensor_scalar(sx_clip[:, :, :], sx_pos[:, :, :], 0.0, float(V - 1), ALU.max, ALU.min).then_inc(rows_step, 1)
            dve.wait_ge(rows_step, 3)
            base = field_base[:, :].rearrange("p (a f) -> p a f", a=1)
            nc.vector.tensor_tensor(rows_f[:, :, 0:F], sx_clip[:, :, :], base.broadcast_to([128, C, F]),
                                    ALU.add).then_inc(rows_step, 1)
            nc.vector.tensor_tensor(rows_f[:, :, F:Q], sx_clip[:, :, 0:Q - F],
                                    base[:, :, 0:Q - F].broadcast_to([128, C, Q - F]), ALU.add).then_inc(rows_step, 1)
            dve.wait_ge(rows_turned, 1)
            nc.vector.tensor_copy(rows_now[:, :], x_ps[:, 0:K * H]).then_inc(rows_ready, 1)
            nc.vector.tensor_copy(rows_all[:, :], x_ps[:, 0:128]).then_inc(rows_ready, 1)
            nc.vector.memset(att_diag[:, :, :, :], 0.0).then_inc(zeros_made, 1)

            def spread_first(u):
                dve.wait_ge(first_turned, u + 1)
                src = x_ps[:, 0:128].rearrange("p (c j) -> p c j", j=Q)
                nc.vector.tensor_copy(emb_t[:, 2 * u, :, 0:Q], src).then_inc(first_emb_t_ready, 1)
                nc.vector.tensor_copy(emb_t[:, 2 * u, :, Q:FW], src[:, :, Q - F:FW - F]).then_inc(first_emb_t_ready, 1)

            def spread_second(u):
                dve.wait_ge(turned, u + 1)
                src = tr_ps[:, 128:256].rearrange("p (c j) -> p c j", j=Q)
                nc.vector.tensor_copy(emb_t[:, 2 * u + 1, :, 0:Q], src).then_inc(emb_t_ready, 1)
                nc.vector.tensor_copy(emb_t[:, 2 * u + 1, :, Q:FW], src[:, :, Q - F:FW - F]).then_inc(emb_t_ready, 1)

            def products(t, k):
                n = t * K + k
                opening = isinstance(t, int) and t == 0 and k < 2 * OPENING
                if opening and k % 2 == 0:
                    dve.wait_ge(first_emb_t_ready, k + 2)
                elif opening or k % 2 == 0:
                    dve.wait_ge(emb_t_ready, (t * U + (k // 2 + 1)) * 2)
                if not (isinstance(t, int) and t * K + k < PROD_RING):
                    dve.wait_ge(z_ready, (n - (PROD_RING - 1)) * 2)
                e = emb_t[:, bass.ds(n, 1), :, :].rearrange("p n c j -> p (n c) j")
                row = list(e.ap)
                part, step_c = row[0], row[1]
                left = bass.AP(e.tensor, e.offset, [part, step_c, [0, NDELTA], [1, F]])
                right = bass.AP(e.tensor, e.offset + 1, [part, step_c, [1, NDELTA], [1, F]])
                slot = prod[:, k % PROD_RING, :, :]
                nc.vector.tensor_tensor(slot[:, :, 0:NFULL].rearrange("p c (s i) -> p c s i", i=F), left, right,
                                        ALU.mult).then_inc(prod_ready, 1)
                nc.vector.tensor_tensor(slot[:, :, NFULL:NPAIR], e[:, :, 0:F // 2], e[:, :, F // 2:F],
                                        ALU.mult).then_inc(prod_ready, 1)

            def split_weights():
                dve.wait_ge(att_loaded, N_ATT)
                nc.vector.tensor_copy(att_w_high[:, :], att_w_diag[:, :]).then_inc(w_split, 1)
                for part in (prod_high, prod_low):
                    nc.vector.memset(part[:, :, :, NPAIR:NP2].bitcast(F32), 0.0).then_inc(w_split, 1)
                dve.wait_ge(w_split, 1)
                nc.vector.tensor_tensor(att_w_low[:, :], att_w_diag[:, :], att_w_high[:, :], ALU.subtract).then_inc(w_split, 1)

            def low_part(t, k):
                dve.wait_ge(high_ready, split_count(t, k))
                nc.vector.tensor_tensor(prod_low[:, k % RING, :, 0:NPAIR], prod[:, k % PROD_RING, :, :],
                                        prod_high[:, k % RING, :, 0:NPAIR], ALU.subtract).then_inc(low_ready, 1)

            def maxima(s, rounds, bank):
                dve.wait_ge(scored, rounds)
                nc.vector.tensor_reduce(neg_max[:, 0:1], bank[:, 0:NPAIR], AX.X, ALU.max, negate=True).then_inc(max_step, 1)
                dve.wait_ge(max_step, s * 2 + 1)
                nc.vector.scalar_tensor_tensor(out=neg_max[:, 1:2], in0=neg_max[:, 0:1], scalar=score_bias[:, :],
                                               in1=score_bias[:, :], op0=ALU.subtract, op1=ALU.add).then_inc(max_step, 1)

            def weights(s):
                dve.wait_ge(exp_done, s + 1)
                nc.vector.reciprocal(denom[:, 1:2], denom[:, 0:1]).then_inc(inv_done, 1)
                dve.wait_ge(inv_done, s + 1)
                base = att_skew[:, :, :]
                part = list(base.ap)[0]
                full = bass.AP(base.tensor, base.offset + 1, [part, [1, NDELTA], [FW + 1, F]])
                half = bass.AP(base.tensor, base.offset + F // 2, [part, [FW + 1, F // 2]])
                nc.vector.tensor_scalar(full, expd[:, 0:NFULL].rearrange("p (s i) -> p s i", i=F),
                                        denom[:, 1:2], None, ALU.mult).then_inc(skew_done, 1)
                nc.vector.tensor_scalar(half, expd[:, NFULL:NPAIR], denom[:, 1:2], None, ALU.mult).then_inc(skew_done, 1)
                dve.wait_ge(skew_done, (s + 1) * 2 + 2)
                lo = Q - NDELTA
                nc.vector.tensor_copy(att_skew[:, lo:F, Q - F:FW - F], att_skew[:, lo:F, Q:FW]).then_inc(fold_done, 1)

            def compact(s):
                dve.wait_ge(fold_done, s + 1)
                dve.wait_ge(diag_ready, s * C + 2)
                nc.vector.transpose(att_compact[:, :, :], att_skew[:, :, 0:Q]).then_inc(compact_ready, 1)

            def pooling(t, q, bank):
                dve.wait_ge(g_ready, t * NB + (q + 1))
                dve.wait_ge(pooled_done, t * NB + (q + 1))
                e = emb_t[:, bass.ds(t * K + q * KB, KB), :, 0:F].rearrange("p n c j -> p (n c) j")
                nc.vector.tensor_tensor(pooled_i[:, q % 2, :, :], bank[:, 0:KB * C * F].rearrange("p (x i) -> p x i", i=F), e,
                                        ALU.mult).then_inc(g_used, 1)
                dve.wait_ge(g_used, t * NB + (q + 3))
                nc.vector.tensor_reduce(pooled[:, bass.ds(t * (K * C) + q * (KB * C), KB * C)], pooled_i[:, q % 2, :, :],
                                        AX.X, ALU.add).then_inc(pooled_done, 1)

            def statistics(t):
                dve.wait_ge(pooled_done, (t + 1) * NB + 2)
                cols = bass.ds(t * (K * C), K * C)
                for h in range(H):
                    nc.vector.tensor_copy(feat_h[0:D, h, cols], pooled[h * D:(h + 1) * D, cols]).then_inc(feat_ready, 1)
                dve.wait_ge(feat_ready, (t + 1) * H + 2)
                for h in range(H):
                    last = nc.vector.bn_stats(bn_raw[:, bass.ds(t * H + h, 1), :].rearrange("p a s -> p (a s)"), feat_h[:, h, cols])
                    last.then_inc(stats_done, 1)

            feat_h = feat[:, :].rearrange("p (h n) -> p h n", h=H)

            def body(t, first, last):
                pool_rounds = LAST_POOL_ROUNDS if last else POOL_ROUNDS
                for k in range(K):
                    if first and k < 2 * OPENING:
                        spread_first(k // 2) if k % 2 == 0 else spread_second(k // 2)
                    before = divmod(k - LOW_LATER, K)
                    parted = not (first and k < LOW_LATER) and is_split(t + before[0], before[1])
                    hurry = last and k + 1 == K
                    if parted and hurry:
                        low_part(t + before[0], before[1])
                    products(t, k)
                    if parted and not hurry:
                        low_part(t + before[0], before[1])
                    if first:
                        if k == 2:
                            split_weights()
                        elif k == K - 4:
                            dve.wait_ge(dx_turned, 1)
                            nc.vector.tensor_copy(feat[D:FEA, :].rearrange("p (h n c) -> p h n c", h=H, c=C),
                                                  x_ps[D:FEA, :].rearrange("p (n h c) -> p h n c", h=H, c=C)).then_inc(feat_ready, 2)
                        continue
                    if k == MAX_AT:
                        maxima(t - 1, t * K, s_ps)
                    if k == MAX_AT + 1:
                        weights(t - 1)
                        compact(t - 1)
                    if k - POOL_LATER in pool_rounds:
                        pooling(t - 1, pool_rounds.index(k - POOL_LATER), g_ps)
                    if k - POOL_LATER - 1 == pool_rounds[-1] and not last:
                        statistics(t - 1)
                    if last and k == PART_ROUNDS + OWN_MAX:
                        maxima(t, t * K + PART_ROUNDS, s_ps)
                    if last and k == PART_ROUNDS + OWN_MAX + 1:
                        weights(t)
                        compact(t)

            blocks(dve, body)
            for k in range(K - LOW_LATER, K):
                if is_split(T - 1, k):
                    low_part(T - 1, k)
            statistics(T - 2)
            for q in range(len(OWN_POOL_ROUNDS)):
                pooling(T - 1, q, g_ps)
            maxima(T, T * K, x_ps)
            dve.wait_ge(diag_ready, T * C + 2)
            weights(T)
            compact(T)
            for c in range(C - 1):
                spread_diagonal(dve, c, nc.vector.tensor_copy)
            for q in range(len(OWN_POOL_ROUNDS), NB):
                pooling(T - 1, q, g_ps if q < PART_BATCHES else z_ps[:, q, :])
            statistics(T - 1)
            dve.wait_ge(stats_done, T * H)
            nc.vector.bn_aggr(bn_mv[:, :], bn_raw[:, :, :].rearrange("p t s -> p (t s)")).then_inc(bn_step, 1)
            dve.wait_ge(std_done, 1)
            dve.wait_ge(dense_loaded, N_DENSE)
            nc.vector.reciprocal(bn_tmp[:, 1:2], bn_tmp[:, 0:1]).then_inc(bn_step, 1)
            dve.wait_ge(bn_step, 2)
            nc.vector.tensor_tensor(bn_tmp[:, 2:3], bn_tmp[:, 1:2], gamma_sb[:, :], ALU.mult).then_inc(bn_step, 1)
            nc.vector.tensor_scalar(bn_tmp[:, 3:4], bn_mv[:, 0:1], -1.0, None, ALU.mult).then_inc(neg_mean, 1)
            dve.wait_ge(neg_mean, 1)
            dve.wait_ge(bn_step, 3)
            nc.vector.scalar_tensor_tensor(out=bn_tmp[:, 4:5], in0=bn_tmp[:, 2:3], scalar=bn_tmp[:, 3:4],
                                           in1=beta_sb[:, :], op0=ALU.mult, op1=ALU.add).then_inc(bn_step, 1)
            dve.wait_ge(bn_step, 4)
            for h in range(H):
                nc.vector.tensor_scalar(feat_n[:, h * BH:(h + 1) * BH], feat[:, h * BH:(h + 1) * BH], bn_tmp[:, 2:3],
                                        bn_tmp[:, 4:5], ALU.mult, ALU.add).then_inc(feat_n_ready[h], 1)

            def relu_bias(dst, src, bias, ready):
                nc.vector.tensor_scalar(dst, src, bias, 0.0, ALU.add, ALU.max).then_inc(ready, 1)

            for h in range(H):
                dve.wait_ge(l1_done[h], 2)
                relu_bias(h1[:, 1, h * BH:(h + 1) * BH], z_ps[:, 2 * h + 1, 0:BH], b1_sb[:, 1:2], h1_ready[h][1])
            dve.wait_ge(l2_done[0], 1)
            relu_bias(h2[:, 0:BH], l2_ps[0][:, 0:BH], b2_sb[:, :], h2_ready[0])
            dve.wait_ge(l3_done[0], 1)
            relu_bias(h3[:, 0:BH], l3_ps[0][0:H3, 0:BH], b3_sb[:, :], h3_ready[0])


_INS = ['r_dx', 'r_sx', 'L0_rec_emb_table', 'L0_rec_att_w_W', 'L0_rec_att_w_b', 'L0_rec_att_d_W',
        'L0_rec_att_d_b', 'L0_rec_bn_gamma', 'L0_rec_bn_beta', 'L0_rec_w1', 'L0_rec_b1', 'L0_rec_w2',
        'L0_rec_b2', 'L0_rec_w3', 'L0_rec_b3', 'L0_rec_wf', 'L0_rec_bf']


def kernel(**inputs):
    import numpy as np
    import concourse.bacc as bacc
    from concourse.bass_utils import run_bass_kernel_spmd

    nc = bacc.Bacc("TRN2", target_bir_lowering=False, num_devices=1)
    arrays, args = {}, []
    for name in _INS:
        a = np.ascontiguousarray(inputs[name])
        arrays[f"in_{name}"] = a
        args.append(nc.dram_tensor(f"in_{name}", a.shape, mybir.dt.from_np(a.dtype), kind="ExternalInput").ap())
    args.append(nc.dram_tensor("out_prob", (B,), F32, kind="ExternalOutput").ap())
    afm_kernel(nc, *args)
    r = run_bass_kernel_spmd(nc, [arrays], core_ids=[0])
    return r.results[0]["out_prob"]
```
